# Optimizing a Trainium2 kernel written in Bass

```python
import numpy as np
import jax
import jax.numpy as jnp

def _softmax(x, axis=-1):
    return jax.nn.softmax(x, axis=axis)

def _gelu(x):
    return jax.nn.gelu(x, approximate=True)

def _silu(x):
    return jax.nn.silu(x)

def _sigmoid(x):
    return jax.nn.sigmoid(x)

def _layernorm(x, axis=-1, eps=1e-05):
    m = jnp.mean(x, axis=axis, keepdims=True)
    v = jnp.var(x, axis=axis, keepdims=True)
    return (x - m) / jnp.sqrt(v + eps)

def _scatter_add(tgt, idx, src, axis=0):
    return tgt.at[idx].add(src)

def _segment_sum(src, seg, n):
    return jax.ops.segment_sum(src, seg, n)
kernel_name = 'mk_gnn_preln_d1_gnn_r8_f1d2cb'

def setup_inputs(seed: int=0):
    np.random.seed(seed)
    _w = jnp.asarray

    def _rec_inputs():
        import jax
        import jax.numpy as jnp
        _gk = jax.random.key(seed)
        x = -0.000202 + 1 * jax.random.normal(jax.random.fold_in(_gk, 1), (6250, 128), jnp.float32)
        src = jax.random.randint(jax.random.fold_in(_gk, 2), (100000,), 0, 6250, jnp.int32)
        dst = jax.random.randint(jax.random.fold_in(_gk, 3), (100000,), 0, 6250, jnp.int32)
        _o = jnp.argsort(dst, stable=True)
        src = src[_o]
        dst = dst[_o]
        edge_attr_128 = -8.16379e-05 + 0.999858 * jax.random.normal(jax.random.fold_in(_gk, 12), (100000, 128), jnp.float32)
        return (x, src, dst, edge_attr_128)
    x, src, dst, edge_attr_128 = _rec_inputs()

    def _L0_gnn_setup():
        import jax, jax.numpy as jnp
        import numpy as np
        N_NODES = 6250
        N_EDGES = 100000
        NODE_DIM = 128
        EDGE_DIM = 128
        OUT_FEATS = 128
        key = jax.random.key(seed)
        k1, k2, k3, k4, k5, k6 = jax.random.split(key, 6)
        node_features = jax.random.normal(k1, (N_NODES, NODE_DIM), dtype=jnp.float32)
        edge_features = jax.random.normal(k2, (N_EDGES, EDGE_DIM), dtype=jnp.float32)
        src = jax.random.randint(k3, (N_EDGES,), 0, N_NODES, dtype=jnp.int32)
        dst = jax.random.randint(k4, (N_EDGES,), 0, N_NODES, dtype=jnp.int32)
        in_dim = 2 * NODE_DIM + EDGE_DIM
        W = jax.random.normal(k5, (OUT_FEATS, in_dim), dtype=jnp.float32) / np.sqrt(in_dim)
        b = jax.random.normal(k6, (OUT_FEATS,), dtype=jnp.float32) * 0.01
        return {'node_features': node_features, 'edge_features': edge_features, 'src': src, 'dst': dst, 'W': W, 'b': b}
    _L0_gnn_all = _L0_gnn_setup()
    _L0_gnn_in = {k: v for k, v in _L0_gnn_all.items() if k in ('W', 'b')}
    del _L0_gnn_all
    return {'x': x, 'src': src, 'dst': dst, 'edge_attr_128': edge_attr_128, 'L0_gnn_W': _L0_gnn_in['W'], 'L0_gnn_b': _L0_gnn_in['b']}

def reference(x, src, dst, edge_attr_128, L0_gnn_W, L0_gnn_b):
    import jax
    import jax.numpy as jnp

    def _L0_gnn_ref(node_features, edge_features, src, dst, W, b):
        import jax, jax.numpy as jnp
        import numpy as np
        N_NODES = 6250
        N_EDGES = 100000
        NODE_DIM = 128
        EDGE_DIM = 128
        OUT_FEATS = 128
        agg_src = jax.ops.segment_sum(node_features[src], dst, num_segments=N_NODES)
        agg_edge = jax.ops.segment_sum(edge_features, dst, num_segments=N_NODES)
        h = jnp.concatenate([node_features, agg_src, agg_edge], axis=1)
        h = h @ W.T + b
        return jax.nn.relu(h)
    h = jnp.maximum(_layernorm(x, axis=-1), 0.0)
    x = x + _L0_gnn_ref(h, edge_attr_128, src, dst, L0_gnn_W, L0_gnn_b)
    return x

_drawn_inputs = setup_inputs


def setup_inputs(seed=0):
    import zlib

    import numpy as np

    out = dict(_drawn_inputs(seed))
    spreads = {}
    factors = {'L0_gnn_b': 25.993}
    for name, (base, spread) in spreads.items():
        noise = np.random.default_rng([zlib.crc32(name.encode()), seed]).standard_normal(out[name].shape)
        drawn = base * np.exp(spread * noise) if base else spread * noise
        out[name] = jnp.asarray(drawn.astype(out[name].dtype))
    for name, factor in factors.items():
        out[name] = (out[name] * factor).astype(out[name].dtype)
    return out
```

```python
from contextlib import ExitStack

import concourse.bass as bass
import concourse.mybir as mybir

FP32, BF16, FP16, I32 = mybir.dt.float32, mybir.dt.bfloat16, mybir.dt.float16, mybir.dt.int32
ALU = mybir.AluOpType
ACT = mybir.ActivationFunctionType
AX = mybir.AxisListType
ds = bass.ds

P = 128
N, E, F = 6250, 100000, 128
EPS = 1e-5

NT = -(-N // P)
NLAST = N - (NT - 1) * P
CH = 7
NCH = NT // CH
assert NT == NCH * CH

J = 5
SUB = P * J
ROW = 2 * SUB
TPR = ROW // P
ROWS = E // ROW
TAIL0 = ROWS * ROW
TJ = 2
TP = (E - TAIL0) // TJ
ROWP = ROWS + 1

STEPS = 2
RPS = 3
GRPS = RPS - 1
SPS = 2 * RPS
RPB, SPB = STEPS * RPS, STEPS * SPS
GPB = STEPS * GRPS
BODIES = ROWS // RPB
assert ROWS == BODIES * RPB
CPB = STEPS * TPR
APS = SPS + TPR

WIN = 64
CW = 14
HI = 50
HALF = HI // 2 * CW
PARTS = 3

SLOTS = 3
HOTS = 4
CHOTS = TPR
TURN = 4
assert TURN * BODIES >= NT and RPB % SLOTS == 0 and SPB % HOTS == 0

GW = 448
GWINS = -(-N // GW)
GP, GJ = 125, 5
GSTEPS = E // (GP * GJ)
assert GSTEPS * GP * GJ == E
ACCW = max(GW * GWINS, N + WIN)

FB = 4


def gnn_program(nc, x, src, dst, edge, W, b, out):
    nc.disable_value_cache = True
    ctx = ExitStack()
    with ctx:
        def sb(name, shape, dt):
            return ctx.enter_context(nc.sbuf_tensor(name, shape, dt))

        def sem(name):
            return ctx.enter_context(nc.semaphore(name))

        h_dram = nc.dram_tensor("h_table", [N, F], FP32, kind="Internal").ap()

        h = sb("h", [P, TURN * BODIES, F], FP32)
        acc = sb("acc", [P, 2, ACCW], FP32)
        parts = sb("parts", [P, PARTS, NT, F], BF16)
        staged = sb("staged", [P, TURN, F], FP32)
        counts = sb("counts", [P, HI, TPR, CW], BF16)
        edge_rows = sb("edge_rows", [P, SLOTS, 2, J * F], FP32)
        gathered = sb("gathered", [P, GPB * 2, J, F], FP32)
        gather_idx = sb("gather_idx", [P, GPB, 2, J], I32)
        hot = sb("hot", [P, HOTS, J, WIN], FP32)
        hot_code = sb("hot_code", [P, CHOTS, 2 * HALF], BF16)
        hot_lo = sb("hot_lo", [P, CHOTS, P], BF16)
        rel_t = sb("rel_t", [P, ROWP * TPR], FP32)
        code_t = sb("code_t", [P, ROWP * TPR], FP32)
        lo_t = sb("lo_t", [P, ROWP * TPR], FP32)
        tile_base = sb("tile_base", [1, TPR * ROWS], I32)
        ident = sb("ident", [P, P], FP32)
        iota_h = sb("iota_h", [P, 2 * HALF], FP16)
        iota_f = sb("iota_f", [P, WIN], FP32)
        w_in = sb("w_in", [P, 3 * F], FP32)
        wt = sb("wt", [P, 3, F], FP32)
        b_all = sb("b_all", [P, F], FP32)
        eps = sb("eps", [P, 1], FP32)
        stats = sb("stats", [P, NT, 6], FP32)
        mv = sb("mv", [P, NT, 2], FP32)
        std = sb("std", [P, NT], FP32)
        rstd = sb("rstd", [P, NT], FP32)
        shift = sb("shift", [P, NT], FP32)
        first_sub = sb("first_sub", [ROWS, 2], FP32)
        first_tile = sb("first_tile", [ROWS, TPR], FP32)
        worst = sb("worst", [P, 8], FP32)
        outside = sb("outside", [P, 2], FP32)
        flag_f = sb("flag_f", [1, 1], FP32)
        flag = sb("flag", [1, 1], I32)
        tail_dst = sb("tail_dst", [TP, TJ], I32)
        tail_first = sb("tail_first", [TP, 1], I32)
        tail_first_f = sb("tail_first_f", [TP, 1], FP32)
        tail_rel = sb("tail_rel", [TP, TJ], FP32)
        tail_idx = sb("tail_idx", [TP, TJ], I32)
        tail_edges = sb("tail_edges", [TP, TJ * F], FP32)
        tail_rows = sb("tail_rows", [TP, TJ, F], FP32)
        tail_hot = sb("tail_hot", [TP, TJ, WIN], FP32)

        lent = counts[:, :, :, :].rearrange("p q t w -> p (q t w)").bitcast(FP32)
        rel_sub = lent[0:ROWS, 0:ROW]
        iota_i = lent[:, ROW:ROW + 2 * HALF].bitcast(I32)
        split = lent[:, ROW + 2 * HALF:ROW + 2 * HALF + CH * F].rearrange("p (t f) -> p t f", f=F)
        dst_f, src_f, lo_f = (edge_rows[0:ROWS, k, :, :].rearrange("p b n -> p (b n)") for k in range(3))
        dst_i, src_i, lo_i = (v.bitcast(I32) for v in (dst_f, src_f, lo_f))

        count_ps = ctx.enter_context(nc.psum_tensor("count_ps", [P, 4, 512], FP32))
        win_ps = ctx.enter_context(nc.psum_tensor("win_ps", [P, 2, 512], FP32))
        apply_ps = ctx.enter_context(nc.psum_tensor("apply_ps", [P, 512], FP32))
        turn_ps = ctx.enter_context(nc.psum_tensor("turn_ps", [P, 512], FP32))

        x_in = [sem(f"x_in{c}") for c in range(NCH)]
        w_ld, ids_in, small_in = sem("w_ld"), sem("ids_in"), sem("small_in")
        zero_tail, consts = sem("zero_tail"), sem("consts")
        iota_done, eye = sem("iota_done"), sem("eye")
        mv_ready, std_ready, scale_ready, h_ready = (sem(n) for n in ("mv_ready", "std_ready", "scale_ready", "h_ready"))
        hi_ready, res_ready, mid_ready, parts_ready = (sem(n) for n in ("hi_ready", "res_ready", "mid_ready", "parts_ready"))
        staged_ready, turned, turn_copied = sem("staged_ready"), sem("turned"), sem("turn_copied")
        h_stored = sem("h_stored")
        dve_step = sem("dve_step")
        ids_ready, ids_t, ids_copied = sem("ids_ready"), sem("ids_t"), sem("ids_copied")
        wt_ps, wt_ready = sem("wt_ps"), sem("wt_ready")
        flag_ps, flag_ready = sem("flag_ps"), sem("flag_ready")
        acc_zero = sem("acc_zero")
        edges_in = [sem(f"edges_in{k}") for k in range(SLOTS)]
        idx_in = [sem(f"idx_in{k}") for k in range(GPB)]
        rows_in = [sem(f"rows_in{k}") for k in range(2 * GPB)]
        hot_ready, subs_done = sem("hot_ready"), sem("subs_done")
        chot_ready, counted, counts_ready = sem("chot_ready"), sem("counted"), sem("counts_ready")
        applied, acc_step = sem("applied"), sem("acc_step")
        gathers_begun = sem("gathers_begun")
        tail_in, tail_gathered, tail_hot_ready = sem("tail_in"), sem("tail_gathered"), sem("tail_hot_ready")
        tail_done, sums_ready = sem("tail_done"), sem("sums_ready")
        g_in, g_rows, g_step, g_hot = sem("g_in"), sem("g_rows"), sem("g_step"), sem("g_hot")
        g_iota, g_open, g_closed, g_saved = sem("g_iota"), sem("g_open"), sem("g_closed"), sem("g_saved")
        g_dve = sem("g_dve")
        x_back = [sem(f"x_back{c}") for c in range(2)]
        last_done, last_sum, last_out, out_ready, stored = (sem(n) for n in ("last_done", "last_sum", "last_out", "out_ready", "stored"))

        def in_use(r):
            return P if r < NT - 1 else NLAST

        def x_tiles(v, t0, t1):
            return v[t0 * P:t1 * P, :].rearrange("(t p) f -> p t f", p=P)

        g_edges = edge_rows[0:GP, 0, 0, :]
        g_gathered = gathered[0:GP, 0, :, :]
        g_idx = gather_idx[0:GP, 0, 0, :]
        g_dst_i = gather_idx[0:GP, 0, 1, :]
        g_dst = stats[0:GP, 0, 0:GJ]
        g_iota_f = lent[:, 0:GW]
        g_hots = lent[0:GP, GW:(1 + GJ) * GW].rearrange("p (j w) -> p j w", j=GJ)
        g_iota_i = gathered[:, 1, :, :].rearrange("p j f -> p (j f)")[:, 0:GW].bitcast(I32)
        g_zero = gathered[0:1, 2, :, :].rearrange("p j f -> p (j f)")[:, 0:GW]

        x_again = parts[:, :, :, :].rearrange("p a t f -> p (a t f)").bitcast(FP32)
        x_again = x_again[:, 0:NT * F].rearrange("p (t f) -> p t f", t=NT)
        groups = [(t, min(t + FB, NT)) for t in range(0, NT, FB)]

        def gathered_rows(r):
            return r % RPS > 0, r // RPS * GRPS + r % RPS - 1

        block = ctx.enter_context(nc.Block())

        @block.sync
        def _(sp):
            for c in range(NCH):
                if c < NCH - 1:
                    sp.dma_start(h[:, c * CH:(c + 1) * CH, :], x_tiles(x, c * CH, (c + 1) * CH)).then_inc(x_in[c], 16)
                else:
                    sp.dma_start(h[:, c * CH:NT - 1, :], x_tiles(x, c * CH, NT - 1)).then_inc(x_in[c], 16)
                    sp.wait_ge(zero_tail, 1)
                    sp.dma_start(h[0:NLAST, NT - 1, :], x[(NT - 1) * P:N, :]).then_inc(x_in[c], 16)
            for c in range(NCH):
                sp.wait_ge(h_ready, c + 1)
                if c < NCH - 1:
                    sp.dma_start(x_tiles(h_dram, c * CH, (c + 1) * CH), h[:, c * CH:(c + 1) * CH, :]).then_inc(h_stored, 16)
                else:
                    sp.dma_start(x_tiles(h_dram, c * CH, NT - 1), h[:, c * CH:NT - 1, :]).then_inc(h_stored, 16)
                    sp.dma_start(h_dram[(NT - 1) * P:N, :], h[0:NLAST, NT - 1, :]).then_inc(h_stored, 16)

            sp.wait_ge(flag_ready, 1)
            sp.wait_ge(ids_t, 6)
            general = sp.value_load(flag[0:1, 0:1], min_val=0, max_val=1)
            with sp.If(general):
                def load(step, n):
                    e0 = sp.snap(step * (GP * GJ))
                    sp.wait_ge(g_step, n + 1)
                    sp.dma_start(g_edges, edge[ds(e0, GP * GJ), :].rearrange("(p j) f -> p (j f)", j=GJ)).then_inc(g_in, 16)
                    sp.dma_start(g_idx, src[ds(e0, GP * GJ)].rearrange("(p j) -> p j", j=GJ)).then_inc(g_in, 16)
                    sp.dma_start(g_dst_i, dst[ds(e0, GP * GJ)].rearrange("(p j) -> p j", j=GJ)).then_inc(g_in, 16)
                with sp.Fori(0, GWINS) as v:
                    with sp.Fori(0, GSTEPS) as step:
                        load(step, v * GSTEPS + step)
            with sp.Else():
                sp.dma_start(tail_edges[:, :], edge[TAIL0:E, :].rearrange("(p j) f -> p (j f)", j=TJ)).then_inc(tail_in, 16)
                def load_indices(row, r):
                    k = gathered_rows(r)[1]
                    ids = src[ds(row * ROW, ROW)].rearrange("(b p j) -> p b j", b=2, j=J)
                    sp.dma_start(gather_idx[:, k, :, :], ids).then_inc(idx_in[k], 16)
                ahead = [r for r in range(SLOTS) if gathered_rows(r)[0]]
                for r in ahead:
                    load_indices(r, r)
                with sp.Fori(0, BODIES) as i:
                    for r in range(RPB):
                        row = sp.snap(i * RPB + r)
                        sp.wait_ge(subs_done, i * SPB + 2 * (r - SLOTS + 1) + SPB)
                        rows = edge[ds(row * ROW, ROW), :].rearrange("(b p j) f -> p b (j f)", b=2, j=J)
                        sp.dma_start(edge_rows[:, r % SLOTS, :, :], rows).then_inc(edges_in[r % SLOTS], 16)
                        if gathered_rows((r + SLOTS) % RPB)[0]:
                            load_indices((row + SLOTS) % ROWS, (r + SLOTS) % RPB)
                for r in ahead:
                    sp.wait_ge(idx_in[gathered_rows(r)[1]], 16 * (BODIES + 1))

            sp.wait_ge(sums_ready, 1)
            half = NT // 2
            sp.dma_start(x_again[:, 0:half, :], x_tiles(x, 0, half)).then_inc(x_back[0], 16)
            sp.dma_start(x_again[:, half:NT - 1, :], x_tiles(x, half, NT - 1)).then_inc(x_back[1], 16)
            sp.dma_start(x_again[0:NLAST, NT - 1, :], x[(NT - 1) * P:N, :]).then_inc(x_back[1], 16)
            for g, (t0, t1) in enumerate(groups):
                sp.wait_ge(out_ready, g + 1)
                if t1 < NT:
                    sp.dma_start(x_tiles(out, t0, t1), h[:, t0:t1, :]).then_inc(stored, 16)
                else:
                    assert t1 - t0 == 1
                    sp.dma_start(out[t0 * P:N, :], h[0:NLAST, t0, :]).then_inc(stored, 16)
            sp.wait_ge(stored, 16 * len(groups))

        @block.gpsimd
        def _(pool):
            pool.memset(ident[:, :], 0.0).then_inc(eye, 1)
            pool.wait_ge(eye, 1)
            pool.affine_select(out=ident[:, :], in_=ident[:, :], compare_op=ALU.not_equal, fill=1.0, base=0,
                               pattern=[[-1, P]], channel_multiplier=1).then_inc(eye, 1)
            pool.iota(iota_i, pattern=[[1, 2 * HALF]], base=0, channel_multiplier=0).then_inc(iota_done, 1)
            pool.memset(acc[:, :, :], 0.0).then_inc(acc_zero, 1)

            pool.wait_ge(flag_ready, 1)
            pool.wait_ge(h_stored, 16 * (NCH + 1))
            general = pool.value_load(flag[0:1, 0:1], min_val=0, max_val=1)
            with pool.If(general):
                pool.iota(g_iota_i, pattern=[[1, GW]], base=0, channel_multiplier=0).then_inc(g_iota, 1)
                pool.memset(g_zero, 0.0).then_inc(g_iota, 1)

                def gather(n):
                    pool.wait_ge(g_in, 48 * (n + 1))
                    pool.sem_inc(gathers_begun, 1)
                    for j in range(GJ):
                        pool.indirect_dma_start(g_gathered[:, j, :], None, h_dram,
                                                bass.IndirectOffsetOnAxis(ap=g_idx[:, j:j + 1], axis=0)).then_inc(g_rows, 16)
                with pool.Fori(0, GWINS) as v:
                    with pool.Fori(0, GSTEPS) as step:
                        gather(v * GSTEPS + step)
            with pool.Else():
                with pool.Fori(0, BODIES) as i:
                    for k in range(GPB):
                        pool.wait_ge(idx_in[k], (i + 1) * 16)
                        pool.sem_inc(gathers_begun, 1)
                        for q in range(2):
                            for j in range(J):
                                pool.indirect_dma_start(
                                    gathered[:, 2 * k + q, j, :], None, h_dram,
                                    bass.IndirectOffsetOnAxis(ap=gather_idx[:, k, q, j:j + 1], axis=0),
                                ).then_inc(rows_in[2 * k + q], 16)
                pool.wait_ge(small_in, 16 * 4)
                for j in range(TJ):
                    pool.indirect_dma_start(tail_rows[:, j, :], None, h_dram,
                                            bass.IndirectOffsetOnAxis(ap=tail_idx[:, j:j + 1], axis=0)).then_inc(tail_gathered, 16)

        @block.scalar
        def _(act):
            act.dma_start(dst_i, dst[0:TAIL0].rearrange("(r n) -> r n", n=ROW)).then_inc(ids_in, 16)
            act.dma_start(src_i, src[0:TAIL0].rearrange("(r n) -> r n", n=ROW)).then_inc(ids_in, 16)
            act.dma_start(w_in[:, :], W[:, :]).then_inc(w_ld, 16)
            act.dma_start(b_all[:, :], b.rearrange("(a n) -> a n", a=1).to_broadcast([P, F])).then_inc(w_ld, 16)
            act.dma_start(tail_dst[:, :], dst[TAIL0:E].rearrange("(p j) -> p j", j=TJ)).then_inc(small_in, 16)
            act.dma_start(tail_idx[:, :], src[TAIL0:E].rearrange("(p j) -> p j", j=TJ)).then_inc(small_in, 16)
            act.dma_start(tail_first[:, :], dst[TAIL0:TAIL0 + 1].rearrange("(a n) -> a n", a=1).to_broadcast([TP, 1])).then_inc(small_in, 16)
            act.dma_start(tile_base[:, :], dst[0:TAIL0].rearrange("(a s n) -> a s n", a=1, n=P)[:, :, 0],
                          allow_slow_non_contiguous=True).then_inc(small_in, 16)

            act.wait_ge(consts, 1)
            def root(c):
                act.wait_ge(mv_ready, c + 1)
                tiles = slice(c * CH, (c + 1) * CH)
                act.activation(std[:, tiles], mv[:, tiles, 1], ACT.Sqrt, bias=eps[:, 0:1]).then_inc(std_ready, 1)
            root(0)
            for c in range(NCH):
                if c + 1 < NCH:
                    root(c + 1)
                act.wait_ge(scale_ready, c + 1)
                for t in range(c * CH, (c + 1) * CH):
                    last = act.activation(h[:, t, :], h[:, t, :], ACT.Relu, bias=shift[:, t:t + 1], scale=rstd[:, t:t + 1])
                last.then_inc(h_ready, 1)
            act.wait_ge(wt_ps, 1)
            act.copy(wt[:, :, :], win_ps[:, 0, 0:3 * F].rearrange("p (k f) -> p k f", k=3)).then_inc(wt_ready, 1)
            for n, arr in enumerate((rel_t, rel_t, code_t, code_t, lo_t, lo_t)):
                act.wait_ge(ids_t, n + 1)
                o = arr[:, 0:ROWS * TPR].rearrange("p (r c) -> p c r", c=TPR)[:, (n % 2) * J:(n % 2) * J + J, :]
                act.copy(o, count_ps[:, n % 4, 0:J * ROWS].rearrange("p (c r) -> p c r", r=ROWS)).then_inc(ids_copied, 1)
            for c in range(NCH):
                tiles = slice(c * CH, (c + 1) * CH)
                act.wait_ge(h_ready, c + 1)
                act.copy(parts[:, 0, tiles, :], h[:, tiles, :]).then_inc(hi_ready, 1)
                act.wait_ge(res_ready, c + 1)
                act.copy(parts[:, 1, tiles, :], split).then_inc(mid_ready, 1)

            act.wait_ge(h_stored, 16 * (NCH + 1))
            act.wait_ge(parts_ready, NCH)
            act.wait_ge(flag_ready, 1)
            general = act.value_load(flag[0:1, 0:1], min_val=0, max_val=1)

            def stage(i):
                act.wait_ge(turned, i + 1)
                act.copy(staged[:, :, :], h[:, ds(i * TURN, TURN), :]).then_inc(staged_ready, 1)

            def copy_turned(i):
                act.wait_ge(turned, i + 2)
                act.copy(h[:, ds(i * TURN, TURN), :], turn_ps[:, :].rearrange("p (t f) -> p t f", f=F)).then_inc(turn_copied, 1)
            with act.If(general):
                with act.Fori(0, BODIES) as i:
                    stage(i)
                    copy_turned(i)
            with act.Else():
                with act.Fori(0, BODIES) as i:
                    for q in range(STEPS):
                        act.wait_ge(applied, i * STEPS + q + 1)
                        for c in range(TPR):
                            act.wait_ge(counted, i * CPB + q * TPR + c + 1 + CHOTS)
                            act.copy(counts[:, :, c, :].rearrange("p (a q) w -> p a q w", a=2),
                                     count_ps[:, 2 * (c % 2):2 * (c % 2) + 2, 0:HALF].rearrange("p a (q w) -> p a q w", w=CW)
                                     ).then_inc(counts_ready, 1)
                        if q == 0:
                            stage(i)
                    copy_turned(i)

        @block.vector
        def _(dve):
            steps = 0

            def link(instruction):
                nonlocal steps
                steps += 1
                instruction.then_inc(dve_step, 1)
                dve.wait_ge(dve_step, steps)

            dve.memset(h[:, NT - 1:, :], 0.0).then_inc(zero_tail, 1)
            dve.memset(eps[:, :], EPS).then_inc(consts, 1)
            dve.memset(outside[:, :], -1.0)
            dve.memset(code_t[:, ROWS * TPR:], 0.0)
            dve.memset(lo_t[:, ROWS * TPR:], 0.0)
            link(dve.memset(rel_t[:, ROWS * TPR:], 0.0))

            def moments(c):
                dve.wait_ge(x_in[c], 16 if c < NCH - 1 else 32)
                for t in range(c * CH, (c + 1) * CH):
                    last = dve.bn_stats(stats[:, t, :], h[:, t, :])
                link(last)
                for t in range(c * CH, (c + 1) * CH):
                    last = dve.bn_aggr(mv[:, t, :], stats[:, t, :])
                last.then_inc(mv_ready, 1)

            def scales(c):
                tiles = slice(c * CH, (c + 1) * CH)
                dve.wait_ge(std_ready, c + 1)
                link(dve.reciprocal(rstd[:, tiles], std[:, tiles]))
                dve.scalar_tensor_tensor(out=shift[:, tiles], in0=mv[:, tiles, 0], scalar=-1.0, in1=rstd[:, tiles],
                                         op0=ALU.mult, op1=ALU.mult).then_inc(scale_ready, 1)
            moments(0)
            for c in range(NCH):
                if c + 1 < NCH:
                    moments(c + 1)
                scales(c)

            dve.wait_ge(iota_done, 1)
            dve.tensor_copy(iota_h[:, :], iota_i)
            link(dve.tensor_copy(iota_f[:, :], iota_i[:, 0:WIN]))

            dve.wait_ge(ids_in, 32)
            link(dve.tensor_copy(dst_f, dst_i))
            dve.tensor_copy(first_sub[:, :], dst_f.rearrange("r (s n) -> r s n", n=SUB)[:, :, 0])
            link(dve.tensor_copy(first_tile[:, :], dst_f.rearrange("r (s n) -> r s n", n=P)[:, :, 0]))
            link(dve.tensor_tensor(rel_sub.rearrange("r (s n) -> r s n", n=SUB), dst_f.rearrange("r (s n) -> r s n", n=SUB),
                                   first_sub[:, :].unsqueeze(2).to_broadcast([ROWS, 2, SUB]), ALU.subtract))
            dve.sem_inc(ids_ready, 1)
            rel3 = dst_f.rearrange("r (s n) -> r s n", n=P)
            link(dve.tensor_tensor(rel3, rel3, first_tile[:, :].unsqueeze(2).to_broadcast([ROWS, TPR, P]), ALU.subtract))
            link(dve.tensor_scalar(lo_i, src_i, P - 1, None, ALU.bitwise_and))
            dve.tensor_copy(lo_f, lo_i)
            link(dve.tensor_copy(src_f, src_i))
            link(dve.tensor_tensor(src_f, src_f, lo_f, ALU.subtract))
            link(dve.scalar_tensor_tensor(out=src_f, in0=src_f, scalar=CW / P, in1=dst_f, op0=ALU.mult, op1=ALU.add))
            dve.sem_inc(ids_ready, 1)

            dve.tensor_reduce(worst[0:ROWS, 0:1], rel_sub, AX.X, ALU.max)
            dve.tensor_reduce(worst[0:ROWS, 1:2], rel_sub, AX.X, ALU.min)
            dve.tensor_reduce(worst[0:ROWS, 2:3], dst_f, AX.X, ALU.max)
            link(dve.tensor_reduce(worst[0:ROWS, 3:4], dst_f, AX.X, ALU.min))
            dve.tensor_scalar(worst[0:ROWS, 4:5], worst[0:ROWS, 0:1], float(WIN) - 0.5, None, ALU.subtract)
            dve.tensor_scalar(worst[0:ROWS, 5:6], worst[0:ROWS, 2:3], float(CW) - 0.5, None, ALU.subtract)
            link(dve.tensor_tensor(worst[0:ROWS, 6:7], worst[0:ROWS, 1:2], worst[0:ROWS, 3:4], ALU.min))
            dve.tensor_tensor(worst[0:ROWS, 4:5], worst[0:ROWS, 4:5], worst[0:ROWS, 5:6], ALU.max)
            link(dve.tensor_scalar(worst[0:ROWS, 6:7], worst[0:ROWS, 6:7], -1.0, -0.5, ALU.mult, ALU.add))
            link(dve.tensor_tensor(outside[0:ROWS, 0:1], worst[0:ROWS, 4:5], worst[0:ROWS, 6:7], ALU.max))
            dve.wait_ge(small_in, 16 * 4)
            dve.tensor_copy(tail_rel[:, :], tail_dst[:, :])
            link(dve.tensor_copy(tail_first_f[:, :], tail_first[:, :]))
            link(dve.tensor_scalar(tail_rel[:, :], tail_rel[:, :], tail_first_f[:, 0:1], None, ALU.subtract))
            dve.tensor_reduce(worst[0:TP, 0:1], tail_rel[:, :], AX.X, ALU.max)
            link(dve.tensor_reduce(worst[0:TP, 1:2], tail_rel[:, :], AX.X, ALU.min))
            dve.tensor_scalar(worst[0:TP, 0:1], worst[0:TP, 0:1], float(WIN) - 0.5, None, ALU.subtract)
            link(dve.tensor_scalar(worst[0:TP, 1:2], worst[0:TP, 1:2], -1.0, -0.5, ALU.mult, ALU.add))
            link(dve.tensor_tensor(outside[0:TP, 1:2], worst[0:TP, 0:1], worst[0:TP, 1:2], ALU.max))
            dve.sem_inc(ids_ready, 1)
            dve.wait_ge(flag_ps, 1)
            link(dve.tensor_reduce(flag_f[:, :], turn_ps[0:1, 0:2 * P], AX.X, ALU.max))
            link(dve.tensor_scalar(flag_f[:, :], flag_f[:, :], 0.0, None, ALU.is_gt))
            dve.tensor_copy(flag[:, :], flag_f[:, :]).then_inc(flag_ready, 1)

            for c in range(NCH):
                tiles = slice(c * CH, (c + 1) * CH)
                dve.wait_ge(hi_ready, c + 1)
                dve.tensor_tensor(split, h[:, tiles, :], parts[:, 0, tiles, :], ALU.subtract).then_inc(res_ready, 1)
                dve.wait_ge(mid_ready, c + 1)
                link(dve.tensor_tensor(parts[:, 2, tiles, :], split, parts[:, 1, tiles, :], ALU.subtract))
                dve.sem_inc(parts_ready, 1)

            dve.wait_ge(flag_ready, 1)
            dve.wait_ge(acc_zero, 1)
            dve.wait_ge(ids_copied, 6)
            general = dve.value_load(flag[0:1, 0:1], min_val=0, max_val=1)
            with dve.If(general):
                dve.wait_ge(g_iota, 2)
                dve.tensor_copy(g_iota_f, g_iota_i).then_inc(g_dve, 1)
                dve.wait_ge(g_dve, 1)

                def one_hots(n):
                    dve.wait_ge(g_in, 48 * (n + 1))
                    dve.wait_ge(g_step, n + 1)
                    dve.tensor_copy(g_dst, g_dst_i).then_inc(g_dve, 1)
                    return n
                with dve.Fori(0, GWINS) as v:
                    with dve.Fori(0, GSTEPS) as step:
                        n = one_hots(v * GSTEPS + step)
                        dve.wait_ge(g_dve, n + v + 2)
                        for j in range(GJ):
                            last = dve.tensor_scalar(g_hots[:, j, :], g_iota_f[0:GP, :], g_dst[:, j:j + 1], None, ALU.is_equal)
                        last.then_inc(g_hot, 1)
                    dve.wait_ge(g_closed, v + 1)
                    dve.tensor_copy(acc[:, :, ds(v * GW, GW)], win_ps[:, :, 0:GW]).then_inc(g_saved, 1)
                    dve.tensor_scalar(g_iota_f, g_iota_f, float(GW), None, ALU.add).then_inc(g_dve, 1)
                    dve.wait_ge(g_dve, (v + 1) * (GSTEPS + 1) + 1)
                dve.sem_inc(sums_ready, 1)
            with dve.Else():
                def sub_hot(n, s):
                    dve.wait_ge(subs_done, n + (SPB - HOTS + 1))
                    rel = rel_t[:, ds(n * J, J)]
                    dve.tensor_tensor(hot[:, s % HOTS, :, :], rel.unsqueeze(2).to_broadcast([P, J, WIN]),
                                      iota_f[:, :].unsqueeze(1).to_broadcast([P, J, WIN]), ALU.is_equal).then_inc(hot_ready, 1)

                def count_hot(i, q, c):
                    t = i * (RPB * TPR) + (q * RPS * TPR + c)
                    dve.wait_ge(counted, i * CPB + (q * TPR + c + 1))
                    dve.tensor_scalar(hot_lo[:, c, :], iota_h[:, 0:P], lo_t[:, ds(t, 1)], None, ALU.is_equal)
                    dve.tensor_scalar(hot_code[:, c, :], iota_h[:, :], code_t[:, ds(t, 1)], None, ALU.is_equal
                                      ).then_inc(chot_ready, 1)

                def bases(ap):
                    return nc.values_load_multi_w_load_instructions(
                        ap, engines=[dve.engine], min_val=0, max_val=N - 1,
                        skip_runtime_bounds_check_because="each is an edge's dst, which names a node")[1]

                def add_sub(i, q, s, n, base):
                    dve.wait_ge(subs_done, i * SPB + (q * SPS + s + SPB + 1))
                    dve.wait_ge(acc_step, i * (STEPS * APS) + ((q + 1) * APS + n))
                    k = 2 if s >= 2 else 1
                    o = acc[:, 0:k, ds(base, WIN)]
                    dve.tensor_tensor(o, o, win_ps[:, s % 2, 0:k * WIN].rearrange("p (k w) -> p k w", k=k), ALU.add
                                      ).then_inc(acc_step, 1)

                def add_tile(i, q, c, n, base):
                    if c == 0:
                        dve.wait_ge(applied, i * STEPS + q + 2)
                    o = acc[:, 1, ds(base, CW)]
                    dve.wait_ge(acc_step, i * (STEPS * APS) + ((q + 1) * APS + n))
                    dve.tensor_tensor(o, o, apply_ps[:, c * CW:(c + 1) * CW], ALU.add).then_inc(acc_step, 1)

                dve.sem_inc(acc_step, APS)
                for s in range(2):
                    sub_hot(s, s)
                for c in range(4):
                    count_hot(0, 0, c)
                with dve.Fori(0, BODIES) as i:
                    for q in range(STEPS):
                        s0 = q * SPS
                        first = bases(tile_base[0:1, ds((i * SPB + s0) * J, SPS * J)].rearrange("a (s j) -> a s j", j=J)[:, :, 0])
                        for s, (c0, c1) in enumerate(((4, 7), (7, 10), (10, 10), (10, 10))):
                            sub_hot(i * SPB + (s0 + s + 2), s0 + s + 2)
                            for c in range(c0, c1):
                                count_hot(i, q, c)
                            add_sub(i, q, s, s, first[s])
                        tiles = bases(tile_base[0:1, ds((i * RPB + q * RPS) * TPR, TPR)])
                        n = 4
                        for c in range(TPR):
                            if c % 5 == 0:
                                sub_hot(i * SPB + (s0 + 6 + c // 5), s0 + 6 + c // 5)
                            add_tile(i, q, c, n, tiles[c])
                            n += 1
                            if c % 5 in (0, 2):
                                count_hot(i, q + 1, c // 5 * 2 + c % 5 // 2)
                            if c % 5 == 4:
                                add_sub(i, q, 4 + c // 5, n, first[4 + c // 5])
                                n += 1
                dve.tensor_tensor(tail_hot[:, :, :], tail_rel[:, :].unsqueeze(2).to_broadcast([TP, TJ, WIN]),
                                  iota_f[0:TP, :].unsqueeze(1).to_broadcast([TP, TJ, WIN]), ALU.is_equal).then_inc(tail_hot_ready, 1)
                base = dve.value_load(tail_first[0:1, 0:1], min_val=0, max_val=N - 1)
                dve.wait_ge(tail_done, 1)
                dve.wait_ge(acc_step, (BODIES * STEPS + 1) * APS)
                o = acc[:, :, ds(base, WIN)]
                dve.tensor_tensor(o, o, win_ps[:, 0, 0:2 * WIN].rearrange("p (k w) -> p k w", k=2), ALU.add).then_inc(sums_ready, 1)

            for g, (t0, t1) in enumerate(groups):
                w = (t1 - t0) * F
                rows = in_use(t1 - 1)
                if g == 0:
                    dve.wait_ge(x_back[0], 16)
                if t1 > NT // 2:
                    dve.wait_ge(x_back[1], 32)
                dve.wait_ge(last_done, g + 1)
                hg = h[0:rows, t0:t1, :]
                dve.tensor_tensor(hg, count_ps[0:rows, g % 4, 0:w].rearrange("p (t f) -> p t f", f=F),
                                  b_all[0:rows, :].unsqueeze(1).to_broadcast([rows, t1 - t0, F]), ALU.add).then_inc(last_sum, 1)
                dve.wait_ge(last_sum, g + 1)
                dve.scalar_tensor_tensor(out=hg, in0=hg, scalar=0.0, in1=x_again[0:rows, t0:t1, :],
                                         op0=ALU.max, op1=ALU.add).then_inc(out_ready, 1)

        @block.tensor
        def _(pe):
            pe.wait_ge(eye, 2)
            pe.wait_ge(w_ld, 32)
            for k in range(3):
                last = pe.transpose(win_ps[:, 0, k * F:(k + 1) * F], w_in[:, k * F:(k + 1) * F], ident[:, :])
            last.then_inc(wt_ps, 1)

            def ids_out(n, c):
                return count_ps[:, n % 4, c * ROWS:(c + 1) * ROWS]
            eye_r = ident[0:ROWS, 0:ROWS]
            pe.wait_ge(ids_ready, 1)
            for q in range(2):
                view = rel_sub[:, q * SUB:(q + 1) * SUB].rearrange("r (p j) -> r j p", j=J)
                for j in range(J):
                    last = pe.transpose(ids_out(q, j), view[:, j, :], eye_r)
                last.then_inc(ids_t, 1)
            pe.wait_ge(ids_ready, 2)
            for n, arr in ((2, src_f), (3, src_f), (4, lo_f), (5, lo_f)):
                if n >= 4:
                    pe.wait_ge(ids_copied, n - 3)
                for c in range(J):
                    at = (n % 2) * J + c
                    last = pe.transpose(ids_out(n, c), arr[:, at * P:(at + 1) * P], eye_r)
                last.then_inc(ids_t, 1)
            pe.wait_ge(ids_ready, 3)
            for k in range(2):
                last = pe.transpose(turn_ps[0:1, k * P:(k + 1) * P], outside[:, k:k + 1], ident[:, :])
            last.then_inc(flag_ps, 1)

            pe.wait_ge(wt_ready, 1)
            pe.wait_ge(ids_copied, 6)

            def turn(i):
                pe.wait_ge(staged_ready, i + 1)
                pe.wait_ge(turn_copied, i + 1)
                for k in range(TURN):
                    last = pe.transpose(turn_ps[:, k * P:(k + 1) * P], staged[:, k, :], ident[:, :])
                last.then_inc(turned, 1)

            pe.wait_ge(flag_ready, 1)
            general = pe.value_load(flag[0:1, 0:1], min_val=0, max_val=1)
            pe.sem_inc(turn_copied, 1)
            pe.sem_inc(turned, 1)
            with pe.If(general):
                pe.wait_ge(parts_ready, NCH)
                with pe.Fori(0, BODIES) as i:
                    turn(i)
                pe.wait_ge(g_iota, 2)
                pe.sem_inc(g_step, 1)

                def products(n):
                    pe.wait_ge(g_in, 48 * (n + 1))
                    pe.wait_ge(g_rows, 16 * GJ * (n + 1))
                    pe.wait_ge(g_hot, n + 1)
                    for j in range(GJ):
                        pe.matmul(win_ps[:, 0, 0:GW], g_edges[:, j * F:(j + 1) * F], g_hots[:, j, :], start=False, stop=False)
                        last = pe.matmul(win_ps[:, 1, 0:GW], g_gathered[:, j, :], g_hots[:, j, :], start=False, stop=False)
                    last.then_inc(g_step, 1)
                pe.sem_inc(g_saved, 1)
                with pe.Fori(0, GWINS) as v:
                    pe.wait_ge(g_saved, v + 1)
                    for k in range(2):
                        pe.matmul(win_ps[:, k, 0:GW], g_zero[:, 0:P], g_zero[:, :], start=True, stop=False)
                    with pe.Fori(0, GSTEPS) as step:
                        products(v * GSTEPS + step)
                    for k in range(2):
                        last = pe.matmul(win_ps[:, k, 0:GW], g_zero[:, 0:P], g_zero[:, :], start=False, stop=True)
                    last.then_inc(g_closed, 1)
            with pe.Else():
                pe.sem_inc(subs_done, SPB)
                pe.sem_inc(counted, CHOTS)
                pe.sem_inc(applied, 1)
                pe.sem_inc(counts_ready, 2)

                def sub_block(i, q, s):
                    r, n = q * RPS + s // 2, q * SPS + s
                    if s % 2 == 0:
                        pe.wait_ge(edges_in[r % SLOTS], i * (RPB // SLOTS * 16) + (r // SLOTS + 1) * 16)
                    pe.wait_ge(hot_ready, i * SPB + (n + 1))
                    pe.wait_ge(acc_step, i * (STEPS * APS) + (adds_through(n - 2) + APS))
                    for j in range(J):
                        last = pe.matmul(win_ps[:, n % 2, 0:WIN], edge_rows[:, r % SLOTS, s % 2, j * F:(j + 1) * F],
                                         hot[:, n % HOTS, j, :], start=j == 0, stop=j == J - 1)
                    if s >= 2:
                        k = 2 * gathered_rows(r)[1] + s % 2
                        pe.wait_ge(rows_in[k], i * (16 * J) + 16 * J)
                        for j in range(J):
                            last = pe.matmul(win_ps[:, n % 2, WIN:2 * WIN], gathered[:, k, j, :], hot[:, n % HOTS, j, :],
                                             start=j == 0, stop=j == J - 1)
                    last.then_inc(subs_done, 1)

                def count(i, q, c):
                    pe.wait_ge(chot_ready, i * CPB + (q * TPR + c + 1))
                    pe.wait_ge(counts_ready, i * CPB + (q * TPR + c + 1))
                    for k in range(2):
                        last = pe.matmul(count_ps[:, 2 * (c % 2) + k, 0:HALF], hot_lo[:, c, :],
                                         hot_code[:, c, k * HALF:(k + 1) * HALF], start=True, stop=True)
                    last.then_inc(counted, 1)

                def apply(i, q):
                    pe.wait_ge(counts_ready, i * CPB + (q + 1) * TPR + 2)
                    pe.wait_ge(parts_ready, NCH)
                    pe.wait_ge(acc_step, i * (STEPS * APS) + (adds_through(q * SPS - 1) + APS))
                    for m in range(NT * PARTS):
                        last = pe.matmul(apply_ps[:, 0:TPR * CW], parts[:, m % PARTS, m // PARTS, :],
                                         counts[:, m // PARTS, :, :].rearrange("p t w -> p (t w)"),
                                         start=m == 0, stop=m == NT * PARTS - 1)
                    last.then_inc(applied, 1)

                with pe.Fori(0, BODIES) as i:
                    for q in range(STEPS):
                        for s, (c0, c1) in enumerate(((0, 4), (4, 7), (7, 10), (10, 10))):
                            for c in range(c0, c1):
                                count(i, q, c)
                            sub_block(i, q, s)
                        apply(i, q)
                        if q == STEPS - 1:
                            turn(i)
                        sub_block(i, q, 4)
                        sub_block(i, q, 5)

                pe.wait_ge(tail_hot_ready, 1)
                pe.wait_ge(tail_in, 16)
                pe.wait_ge(tail_gathered, 16 * TJ)
                for j in range(TJ):
                    pe.matmul(win_ps[:, 0, 0:WIN], tail_edges[:, j * F:(j + 1) * F], tail_hot[:, j, :], start=j == 0, stop=j == TJ - 1)
                for j in range(TJ):
                    last = pe.matmul(win_ps[:, 0, WIN:2 * WIN], tail_rows[:, j, :], tail_hot[:, j, :], start=j == 0, stop=j == TJ - 1)
                last.then_inc(tail_done, 1)

            pe.wait_ge(sums_ready, 1)
            pe.wait_ge(turn_copied, BODIES + 1)
            for g, (t0, t1) in enumerate(groups):
                if g >= 4:
                    pe.wait_ge(last_sum, g - 3)
                for t in range(t0, t1):
                    rows = in_use(t)
                    o = count_ps[0:rows, g % 4, (t - t0) * F:(t - t0 + 1) * F]
                    pe.matmul(o, h[:, t, 0:rows], wt[:, 0, :], start=True, stop=False)
                    pe.matmul(o, acc[:, 0, t * P:t * P + rows], wt[:, 2, :], start=False, stop=False)
                    last = pe.matmul(o, acc[:, 1, t * P:t * P + rows], wt[:, 1, :], start=False, stop=True)
                last.then_inc(last_done, 1)


def adds_through(n):
    q, s = n // SPS, n % SPS
    return q * APS + (s + 1 if s < 4 else s + 1 + (s - 3) * (TPR // 2))


_INS = ["x", "src", "dst", "edge_attr_128", "L0_gnn_W", "L0_gnn_b"]


def kernel(**inputs):
    import numpy as np
    from concourse import bacc
    from concourse.bass_utils import run_bass_kernel_spmd

    nc = bacc.Bacc("TRN2", target_bir_lowering=False, num_devices=1)
    arrays, args = {}, []
    for name in _INS:
        a = np.ascontiguousarray(inputs[name])
        arrays[name] = a
        args.append(nc.dram_tensor(name, a.shape, mybir.dt.from_np(a.dtype), kind="ExternalInput").ap())
    out = nc.dram_tensor("out", (N, F), FP32, kind="ExternalOutput").ap()
    gnn_program(nc, *args, out)
    return run_bass_kernel_spmd(nc, [arrays], core_ids=[0]).results[0]["out"]
```

```python
from contextlib import ExitStack

import concourse.bass as bass
import concourse.mybir as mybir

FP32, BF16, FP16, I32 = mybir.dt.float32, mybir.dt.bfloat16, mybir.dt.float16, mybir.dt.int32
ALU = mybir.AluOpType
ACT = mybir.ActivationFunctionType
AX = mybir.AxisListType
ds = bass.ds

P = 128
N, E, F = 6250, 100000, 128
EPS = 1e-5

NT = -(-N // P)
NLAST = N - (NT - 1) * P
CH = 7
NCH = NT // CH
assert NT == NCH * CH

J = 5
SUB = P * J
ROW = 2 * SUB
TPR = ROW // P
ROWS = E // ROW
TAIL0 = ROWS * ROW
TJ = 2
TP = (E - TAIL0) // TJ
ROWP = ROWS + 2

STEPS = 2
RPS = 3
GRPS = RPS - 1
SPS = 2 * RPS
RPB, SPB = STEPS * RPS, STEPS * SPS
GPB = STEPS * GRPS
BODIES = ROWS // RPB
assert ROWS == BODIES * RPB
CPB = STEPS * TPR
APS = SPS + TPR

WIN = 64
CW = 14
WMID, CMID = (WIN - 1) / 2, (CW - 1) / 2
HI = 50
HALF = HI // 2 * CW
PARTS = 3

SLOTS = 3
HOTS = 6
HOTS_AHEAD = 4
CHOTS = TPR
EARLY = 4
TURN = 4
assert TURN * BODIES >= NT and RPB % SLOTS == 0 and SPB % HOTS == 0

GW = 448
GWINS = -(-N // GW)
GP, GJ = 125, 5
GSTEPS = E // (GP * GJ)
GPARTS = [(v, min(v + 5, GWINS)) for v in range(0, GWINS, 5)]
assert 5 * GSTEPS * GJ * 16 < 2 ** 16
assert GSTEPS * GP * GJ == E
ACCW = max(GW * GWINS, N + WIN)

FB = 4


def gnn_program(nc, x, src, dst, edge, W, b, out):
    nc.disable_value_cache = True
    ctx = ExitStack()
    with ctx:
        def sb(name, shape, dt):
            return ctx.enter_context(nc.sbuf_tensor(name, shape, dt))

        def sem(name):
            return ctx.enter_context(nc.semaphore(name))

        h_dram = nc.dram_tensor("h_table", [N, F], FP32, kind="Internal").ap()

        h = sb("h", [P, TURN * BODIES, F], FP32)
        acc = sb("acc", [P, 2, ACCW], FP32)
        parts = sb("parts", [P, PARTS, NT, F], BF16)
        staged = sb("staged", [P, TURN, F], FP32)
        counts = sb("counts", [P, HI, TPR, CW], BF16)
        edge_rows = sb("edge_rows", [P, SLOTS, 2, J * F], FP32)
        gathered = sb("gathered", [P, GPB * 2, J, F], FP32)
        gather_idx = sb("gather_idx", [P, GPB, 2, J], I32)
        hot = sb("hot", [P, HOTS, J, WIN], FP32)
        hot_code = sb("hot_code", [P, CHOTS, 2 * HALF], BF16)
        hot_lo = sb("hot_lo", [P, CHOTS, P], BF16)
        rel_t = sb("rel_t", [P, ROWP * TPR], FP32)
        code_t = sb("code_t", [P, ROWP * TPR], FP32)
        lo_t = sb("lo_t", [P, ROWP * TPR], FP32)
        tile_base = sb("tile_base", [1, TPR * ROWS], I32)
        ident = sb("ident", [P, P], FP32)
        iota_h = sb("iota_h", [P, 2 * HALF], FP16)
        iota_f = sb("iota_f", [P, WIN], FP32)
        w_in = sb("w_in", [P, 3 * F], FP32)
        wt = sb("wt", [P, 3, F], FP32)
        b_all = sb("b_all", [P, F], FP32)
        eps = sb("eps", [P, 1], FP32)
        stats = sb("stats", [P, NT, 6], FP32)
        mv = sb("mv", [P, NT, 2], FP32)
        std = sb("std", [P, NT], FP32)
        rstd = sb("rstd", [P, NT], FP32)
        shift = sb("shift", [P, NT], FP32)
        first_sub = sb("first_sub", [ROWS, 2], FP32)
        first_tile = sb("first_tile", [ROWS, TPR], FP32)
        worst = sb("worst", [P, 2], FP32)
        outside = sb("outside", [P, 2], FP32)
        flag_f = sb("flag_f", [1, 1], FP32)
        flag = sb("flag", [1, 1], I32)
        tail_dst = sb("tail_dst", [TP, TJ], I32)
        tail_first = sb("tail_first", [TP, 1], I32)
        tail_first_f = sb("tail_first_f", [TP, 1], FP32)
        tail_rel = sb("tail_rel", [TP, TJ], FP32)
        tail_idx = sb("tail_idx", [TP, TJ], I32)
        tail_edges = stats[0:TP, :, :].rearrange("p t k -> p (t k)")[:, 0:TJ * F]
        tail_rows = w_in[0:TP, 0:TJ * F].rearrange("p (j f) -> p j f", j=TJ)
        tail_hot = w_in[0:TP, TJ * F:TJ * (F + WIN)].rearrange("p (j w) -> p j w", j=TJ)

        lent = counts[:, :, :, :].rearrange("p q t w -> p (q t w)").bitcast(FP32)
        rel_sub = lent[0:ROWS, 0:ROW]
        iota_i = lent[:, ROW:ROW + 2 * HALF].bitcast(I32)
        splits = [v.rearrange("p (t f) -> p t f", f=F)
                  for v in (lent[:, ROW + 2 * HALF:ROW + 2 * HALF + CH * F], lent[:, 0:CH * F])]
        dst_f, src_f, lo_f = (edge_rows[0:ROWS, k, :, :].rearrange("p b n -> p (b n)") for k in range(3))
        dst_i, src_i, lo_i = (v.bitcast(I32) for v in (dst_f, src_f, lo_f))

        count_ps = ctx.enter_context(nc.psum_tensor("count_ps", [P, 4, 512], FP32))
        win_ps = ctx.enter_context(nc.psum_tensor("win_ps", [P, 2, 512], FP32))
        apply_ps = ctx.enter_context(nc.psum_tensor("apply_ps", [P, 512], FP32))
        turn_ps = ctx.enter_context(nc.psum_tensor("turn_ps", [P, 512], FP32))

        x_in = [sem(f"x_in{c}") for c in range(NCH)]
        w_ld, ids_in, small_in = sem("w_ld"), sem("ids_in"), sem("small_in")
        zero_tail, consts = sem("zero_tail"), sem("consts")
        iota_done, eye = sem("iota_done"), sem("eye")
        mv_ready, std_ready, scale_ready, h_ready = (sem(n) for n in ("mv_ready", "std_ready", "scale_ready", "h_ready"))
        hi_ready, res_ready, mid_ready, parts_ready = (sem(n) for n in ("hi_ready", "res_ready", "mid_ready", "parts_ready"))
        staged_ready, turned, turn_copied = sem("staged_ready"), sem("turned"), sem("turn_copied")
        h_stored = sem("h_stored")
        dve_step, pool_step = sem("dve_step"), sem("pool_step")
        dst_rel = sem("dst_rel")
        ids_ready, ids_t, ids_copied = sem("ids_ready"), sem("ids_t"), sem("ids_copied")
        wt_ps, wt_ready = sem("wt_ps"), sem("wt_ready")
        flag_ps, flag_ready = sem("flag_ps"), sem("flag_ready")
        acc_zero = sem("acc_zero")
        edges_in = [sem(f"edges_in{k}") for k in range(SLOTS)]
        idx_in = [sem(f"idx_in{k}") for k in range(GPB)]
        rows_in = [sem(f"rows_in{k}") for k in range(2 * GPB)]
        hot_ready, subs_done = sem("hot_ready"), sem("subs_done")
        chot_ready, counted, counts_ready = sem("chot_ready"), sem("counted"), sem("counts_ready")
        applied, acc_step = sem("applied"), sem("acc_step")
        gathers_begun = sem("gathers_begun")
        tail_in, tail_gathered, tail_hot_ready = sem("tail_in"), sem("tail_gathered"), sem("tail_hot_ready")
        tail_done, sums_ready = sem("tail_done"), sem("sums_ready")
        g_in = [sem(f"g_in{k}") for k in range(len(GPARTS))]
        g_rows = [sem(f"g_rows{k}") for k in range(len(GPARTS))]
        g_step, g_hot = sem("g_step"), sem("g_hot")
        g_iota, g_open, g_closed, g_saved = sem("g_iota"), sem("g_open"), sem("g_closed"), sem("g_saved")
        g_dve = sem("g_dve")
        x_back = [sem(f"x_back{c}") for c in range(2)]
        last_done, last_sum, last_out, out_ready, stored = (sem(n) for n in ("last_done", "last_sum", "last_out", "out_ready", "stored"))

        def in_use(r):
            return P if r < NT - 1 else NLAST

        def x_tiles(v, t0, t1):
            return v[t0 * P:t1 * P, :].rearrange("(t p) f -> p t f", p=P)

        g_edges = edge_rows[0:GP, 0, 0, :]
        g_gathered = gathered[0:GP, 0, :, :]
        g_idx = gather_idx[0:GP, 0, 0, :]
        g_dst_i = gather_idx[0:GP, 0, 1, :]
        g_dst = stats[0:GP, 0, 0:GJ]
        g_iota_f = lent[:, 0:GW]
        g_hots = lent[0:GP, GW:(1 + GJ) * GW].rearrange("p (j w) -> p j w", j=GJ)
        g_iota_i = gathered[:, 1, :, :].rearrange("p j f -> p (j f)")[:, 0:GW].bitcast(I32)
        g_zero = gathered[0:1, 2, :, :].rearrange("p j f -> p (j f)")[:, 0:GW]

        x_again = parts[:, :, :, :].rearrange("p a t f -> p (a t f)").bitcast(FP32)
        x_again = x_again[:, 0:NT * F].rearrange("p (t f) -> p t f", t=NT)
        groups = [(t, min(t + FB, NT)) for t in range(0, NT, FB)]

        def gathered_rows(r):
            return r % RPS > 0, r // RPS * GRPS + r % RPS - 1

        block = ctx.enter_context(nc.Block())

        @block.sync
        def _(sp):
            for c in range(NCH):
                if c < NCH - 1:
                    sp.dma_start(h[:, c * CH:(c + 1) * CH, :], x_tiles(x, c * CH, (c + 1) * CH)).then_inc(x_in[c], 16)
                else:
                    sp.dma_start(h[:, c * CH:NT - 1, :], x_tiles(x, c * CH, NT - 1)).then_inc(x_in[c], 16)
                    sp.wait_ge(zero_tail, 1)
                    sp.dma_start(h[0:NLAST, NT - 1, :], x[(NT - 1) * P:N, :]).then_inc(x_in[c], 16)
            for c in range(NCH):
                sp.wait_ge(h_ready, c + 1)
                if c < NCH - 1:
                    sp.dma_start(x_tiles(h_dram, c * CH, (c + 1) * CH), h[:, c * CH:(c + 1) * CH, :]).then_inc(h_stored, 16)
                else:
                    sp.dma_start(x_tiles(h_dram, c * CH, NT - 1), h[:, c * CH:NT - 1, :]).then_inc(h_stored, 16)
                    sp.dma_start(h_dram[(NT - 1) * P:N, :], h[0:NLAST, NT - 1, :]).then_inc(h_stored, 16)

            sp.wait_ge(flag_ready, 1)
            sp.wait_ge(ids_t, 6)
            general = sp.value_load(flag[0:1, 0:1], min_val=0, max_val=1)
            with sp.If(general):
                def load(step, n, g_in):
                    e0 = sp.snap(step * (GP * GJ))
                    sp.wait_ge(g_step, n + 1)
                    sp.dma_start(g_edges, edge[ds(e0, GP * GJ), :].rearrange("(p j) f -> p (j f)", j=GJ)).then_inc(g_in, 16)
                    sp.dma_start(g_idx, src[ds(e0, GP * GJ)].rearrange("(p j) -> p j", j=GJ)).then_inc(g_in, 16)
                    sp.dma_start(g_dst_i, dst[ds(e0, GP * GJ)].rearrange("(p j) -> p j", j=GJ)).then_inc(g_in, 16)
                for k, (v0, v1) in enumerate(GPARTS):
                    with sp.Fori(v0, v1) as v:
                        with sp.Fori(0, GSTEPS) as step:
                            load(step, v * GSTEPS + step, g_in[k])
            with sp.Else():
                sp.dma_start(tail_edges[:, :], edge[TAIL0:E, :].rearrange("(p j) f -> p (j f)", j=TJ)).then_inc(tail_in, 16)
                def load_indices(row, r):
                    k = gathered_rows(r)[1]
                    ids = src[ds(row * ROW, ROW)].rearrange("(b p j) -> p b j", b=2, j=J)
                    sp.dma_start(gather_idx[:, k, :, :], ids).then_inc(idx_in[k], 16)
                ahead = [r for r in range(SLOTS) if gathered_rows(r)[0]]
                for r in ahead:
                    load_indices(r, r)
                with sp.Fori(0, BODIES) as i:
                    for r in range(RPB):
                        row = sp.snap(i * RPB + r)
                        sp.wait_ge(subs_done, i * SPB + 2 * (r - SLOTS + 1) + SPB)
                        rows = edge[ds(row * ROW, ROW), :].rearrange("(b p j) f -> p b (j f)", b=2, j=J)
                        sp.dma_start(edge_rows[:, r % SLOTS, :, :], rows).then_inc(edges_in[r % SLOTS], 16)
                        if gathered_rows((r + SLOTS) % RPB)[0]:
                            load_indices((row + SLOTS) % ROWS, (r + SLOTS) % RPB)
                for r in ahead:
                    sp.wait_ge(idx_in[gathered_rows(r)[1]], 16 * (BODIES + 1))

            sp.wait_ge(sums_ready, 1)
            half = NT // 2
            sp.dma_start(x_again[:, 0:half, :], x_tiles(x, 0, half)).then_inc(x_back[0], 16)
            sp.dma_start(x_again[:, half:NT - 1, :], x_tiles(x, half, NT - 1)).then_inc(x_back[1], 16)
            sp.dma_start(x_again[0:NLAST, NT - 1, :], x[(NT - 1) * P:N, :]).then_inc(x_back[1], 16)
            for g, (t0, t1) in enumerate(groups):
                sp.wait_ge(out_ready, g + 1)
                if t1 < NT:
                    sp.dma_start(x_tiles(out, t0, t1), h[:, t0:t1, :]).then_inc(stored, 16)
                else:
                    assert t1 - t0 == 1
                    sp.dma_start(out[t0 * P:N, :], h[0:NLAST, t0, :]).then_inc(stored, 16)
            sp.wait_ge(stored, 16 * len(groups))

        @block.gpsimd
        def _(pool):
            pool.memset(ident[:, :], 0.0).then_inc(eye, 1)
            pool.wait_ge(eye, 1)
            pool.affine_select(out=ident[:, :], in_=ident[:, :], compare_op=ALU.not_equal, fill=1.0, base=0,
                               pattern=[[-1, P]], channel_multiplier=1).then_inc(eye, 1)
            pool.iota(iota_i, pattern=[[1, 2 * HALF]], base=0, channel_multiplier=0).then_inc(iota_done, 1)
            subs, tiles = (dst_f.rearrange("r (s n) -> r s n", n=n) for n in (SUB, P))
            pool.wait_ge(ids_in, 32)
            pool.tensor_copy(dst_f, dst_i).then_inc(pool_step, 1)
            pool.wait_ge(pool_step, 1)
            pool.tensor_scalar(first_sub[:, :], subs[:, :, 0], WMID, None, ALU.add).then_inc(pool_step, 1)
            pool.tensor_scalar(first_tile[:, :], tiles[:, :, 0], CMID, None, ALU.add).then_inc(pool_step, 1)
            pool.wait_ge(pool_step, 3)
            pool.tensor_tensor(rel_sub.rearrange("r (s n) -> r s n", n=SUB), subs,
                               first_sub[:, :].unsqueeze(2).to_broadcast([ROWS, 2, SUB]), ALU.subtract).then_inc(dst_rel, 1)
            pool.wait_ge(dst_rel, 1)
            pool.tensor_tensor(tiles, tiles, first_tile[:, :].unsqueeze(2).to_broadcast([ROWS, TPR, P]), ALU.subtract
                               ).then_inc(dst_rel, 1)
            pool.memset(acc[:, :, :], 0.0).then_inc(acc_zero, 1)

            pool.wait_ge(flag_ready, 1)
            pool.wait_ge(h_stored, 16 * (NCH + 1))
            general = pool.value_load(flag[0:1, 0:1], min_val=0, max_val=1)
            with pool.If(general):
                pool.iota(g_iota_i, pattern=[[1, GW]], base=0, channel_multiplier=0).then_inc(g_iota, 1)
                pool.memset(g_zero, 0.0).then_inc(g_iota, 1)

                def gather(n, g_in, g_rows):
                    pool.wait_ge(g_in, 48 * (n + 1))
                    pool.sem_inc(gathers_begun, 1)
                    for j in range(GJ):
                        pool.indirect_dma_start(g_gathered[:, j, :], None, h_dram,
                                                bass.IndirectOffsetOnAxis(ap=g_idx[:, j:j + 1], axis=0)).then_inc(g_rows, 16)
                for k, (v0, v1) in enumerate(GPARTS):
                    with pool.Fori(0, v1 - v0) as v:
                        with pool.Fori(0, GSTEPS) as step:
                            gather(v * GSTEPS + step, g_in[k], g_rows[k])
            with pool.Else():
                with pool.Fori(0, BODIES) as i:
                    for k in range(GPB):
                        pool.wait_ge(idx_in[k], (i + 1) * 16)
                        pool.sem_inc(gathers_begun, 1)
                        for q in range(2):
                            for j in range(J):
                                pool.indirect_dma_start(
                                    gathered[:, 2 * k + q, j, :], None, h_dram,
                                    bass.IndirectOffsetOnAxis(ap=gather_idx[:, k, q, j:j + 1], axis=0),
                                ).then_inc(rows_in[2 * k + q], 16)
                pool.wait_ge(small_in, 16 * 4)
                for j in range(TJ):
                    pool.indirect_dma_start(tail_rows[:, j, :], None, h_dram,
                                            bass.IndirectOffsetOnAxis(ap=tail_idx[:, j:j + 1], axis=0)).then_inc(tail_gathered, 16)

        @block.scalar
        def _(act):
            act.dma_start(dst_i, dst[0:TAIL0].rearrange("(r n) -> r n", n=ROW)).then_inc(ids_in, 16)
            act.dma_start(src_i, src[0:TAIL0].rearrange("(r n) -> r n", n=ROW)).then_inc(ids_in, 16)
            act.dma_start(w_in[:, :], W[:, :]).then_inc(w_ld, 16)
            act.dma_start(b_all[:, :], b.rearrange("(a n) -> a n", a=1).to_broadcast([P, F])).then_inc(w_ld, 16)
            act.dma_start(tail_dst[:, :], dst[TAIL0:E].rearrange("(p j) -> p j", j=TJ)).then_inc(small_in, 16)
            act.dma_start(tail_idx[:, :], src[TAIL0:E].rearrange("(p j) -> p j", j=TJ)).then_inc(small_in, 16)
            act.dma_start(tail_first[:, :], dst[TAIL0:TAIL0 + 1].rearrange("(a n) -> a n", a=1).to_broadcast([TP, 1])).then_inc(small_in, 16)
            act.dma_start(tile_base[:, :], dst[0:TAIL0].rearrange("(a s n) -> a s n", a=1, n=P)[:, :, 0],
                          allow_slow_non_contiguous=True).then_inc(small_in, 16)

            act.wait_ge(consts, 1)
            def root(c):
                act.wait_ge(mv_ready, c + 1)
                tiles = slice(c * CH, (c + 1) * CH)
                act.activation(std[:, tiles], mv[:, tiles, 1], ACT.Sqrt, bias=eps[:, 0:1]).then_inc(std_ready, 1)
            root(0)
            for c in range(NCH):
                if c + 1 < NCH:
                    root(c + 1)
                act.wait_ge(scale_ready, c + 1)
                for t in range(c * CH, (c + 1) * CH):
                    last = act.activation(h[:, t, :], h[:, t, :], ACT.Relu, bias=shift[:, t:t + 1], scale=rstd[:, t:t + 1])
                last.then_inc(h_ready, 1)
            act.wait_ge(wt_ps, 1)
            act.copy(wt[:, :, :], win_ps[:, 0, 0:3 * F].rearrange("p (k f) -> p k f", k=3)).then_inc(wt_ready, 1)
            for n, arr in enumerate((rel_t, rel_t, code_t, code_t, lo_t, lo_t)):
                act.wait_ge(ids_t, n + 1)
                o = arr[:, 0:ROWS * TPR].rearrange("p (r c) -> p c r", c=TPR)[:, (n % 2) * J:(n % 2) * J + J, :]
                act.copy(o, count_ps[:, n % 4, 0:J * ROWS].rearrange("p (c r) -> p c r", r=ROWS)).then_inc(ids_copied, 1)
            def first_part(c):
                tiles = slice(c * CH, (c + 1) * CH)
                act.wait_ge(h_ready, c + 1)
                act.copy(parts[:, 0, tiles, :], h[:, tiles, :]).then_inc(hi_ready, 1)
            first_part(0)
            for c in range(NCH):
                if c + 1 < NCH:
                    first_part(c + 1)
                act.wait_ge(res_ready, c + 1)
                act.copy(parts[:, 1, c * CH:(c + 1) * CH, :], splits[c % 2]).then_inc(mid_ready, 1)

            act.wait_ge(h_stored, 16 * (NCH + 1))
            act.wait_ge(parts_ready, NCH)
            act.wait_ge(flag_ready, 1)
            general = act.value_load(flag[0:1, 0:1], min_val=0, max_val=1)

            def stage(i):
                act.wait_ge(turned, i + 1)
                act.copy(staged[:, :, :], h[:, ds(i * TURN, TURN), :]).then_inc(staged_ready, 1)

            def copy_turned(i):
                act.wait_ge(turned, i + 2)
                act.copy(h[:, ds(i * TURN, TURN), :], turn_ps[:, :].rearrange("p (t f) -> p t f", f=F)).then_inc(turn_copied, 1)
            with act.If(general):
                with act.Fori(0, BODIES) as i:
                    stage(i)
                    copy_turned(i)
            with act.Else():
                def copy_counts(i, q, c):
                    act.wait_ge(counted, i * CPB + (q * TPR + c + 1 + CHOTS))
                    act.copy(counts[:, :, c, :].rearrange("p (a q) w -> p a q w", a=2),
                             count_ps[:, 2 * (c % 2):2 * (c % 2) + 2, 0:HALF].rearrange("p a (q w) -> p a q w", w=CW)
                             ).then_inc(counts_ready, 1)
                for c in range(EARLY):
                    copy_counts(0, 0, c)
                with act.Fori(0, BODIES) as i:
                    for q in range(STEPS):
                        for c in range(EARLY, TPR):
                            copy_counts(i, q, c)
                        act.wait_ge(applied, i * STEPS + (q + 2))
                        for c in range(EARLY):
                            copy_counts(i, q + 1, c)
                        if q == 0:
                            stage(i)
                    copy_turned(i)

        @block.vector
        def _(dve):
            steps = 0

            def link(instruction):
                nonlocal steps
                steps += 1
                instruction.then_inc(dve_step, 1)
                dve.wait_ge(dve_step, steps)

            dve.memset(h[:, NT - 1:, :], 0.0).then_inc(zero_tail, 1)
            dve.memset(eps[:, :], EPS).then_inc(consts, 1)
            dve.memset(outside[:, :], -1.0)
            dve.memset(code_t[:, ROWS * TPR:], 0.0)
            dve.memset(lo_t[:, ROWS * TPR:], 0.0)
            link(dve.memset(rel_t[:, ROWS * TPR:], 0.0))

            def moments(c):
                dve.wait_ge(x_in[c], 16 if c < NCH - 1 else 32)
                for t in range(c * CH, (c + 1) * CH):
                    last = dve.bn_stats(stats[:, t, :], h[:, t, :])
                link(last)
                for t in range(c * CH, (c + 1) * CH):
                    last = dve.bn_aggr(mv[:, t, :], stats[:, t, :])
                last.then_inc(mv_ready, 1)

            def scales(c):
                tiles = slice(c * CH, (c + 1) * CH)
                dve.wait_ge(std_ready, c + 1)
                link(dve.reciprocal(rstd[:, tiles], std[:, tiles]))
                dve.scalar_tensor_tensor(out=shift[:, tiles], in0=mv[:, tiles, 0], scalar=-1.0, in1=rstd[:, tiles],
                                         op0=ALU.mult, op1=ALU.mult).then_inc(scale_ready, 1)
            def iotas():
                dve.wait_ge(iota_done, 1)
                dve.tensor_scalar(iota_h[:, :], iota_i, -CMID, None, ALU.add)
                link(dve.tensor_scalar(iota_f[:, :], iota_i[:, 0:WIN], -WMID, None, ALU.add))

            def low():
                dve.wait_ge(ids_in, 32)
                link(dve.tensor_scalar(lo_i, src_i, P - 1, None, ALU.bitwise_and))

            def floats():
                dve.tensor_scalar(lo_f, lo_i, -CMID, None, ALU.add)
                link(dve.tensor_scalar(src_f, src_i, -CMID, None, ALU.add))

            def high():
                link(dve.tensor_tensor(src_f, src_f, lo_f, ALU.subtract))

            def code():
                dve.wait_ge(dst_rel, 2)
                link(dve.scalar_tensor_tensor(out=src_f, in0=src_f, scalar=CW / P, in1=dst_f, op0=ALU.mult, op1=ALU.add))
                dve.sem_inc(ids_ready, 1)

            def far_sub():
                dve.tensor_reduce(worst[0:ROWS, 0:1], rel_sub, AX.X, ALU.max, apply_absolute_value=True)

            def far_tile():
                link(dve.tensor_reduce(worst[0:ROWS, 1:2], dst_f, AX.X, ALU.max, apply_absolute_value=True))
                link(dve.scalar_tensor_tensor(out=outside[0:ROWS, 0:1], in0=worst[0:ROWS, 0:1], scalar=WMID - CMID,
                                              in1=worst[0:ROWS, 1:2], op0=ALU.subtract, op1=ALU.max))
            between = [low, floats, high, iotas, code, far_sub, far_tile]
            moments(0)
            for c in range(NCH):
                if c + 1 < NCH:
                    moments(c + 1)
                scales(c)
                between[c]()
            dve.wait_ge(small_in, 16 * 4)
            dve.tensor_copy(tail_rel[:, :], tail_dst[:, :])
            link(dve.tensor_copy(tail_first_f[:, :], tail_first[:, :]))
            link(dve.tensor_scalar(tail_rel[:, :], tail_rel[:, :], tail_first_f[:, 0:1], WMID, ALU.subtract, ALU.subtract))
            link(dve.tensor_reduce(worst[0:TP, 0:1], tail_rel[:, :], AX.X, ALU.max, apply_absolute_value=True))
            link(dve.tensor_scalar(outside[0:TP, 1:2], worst[0:TP, 0:1], WMID - CMID, None, ALU.subtract))
            dve.sem_inc(ids_ready, 1)
            dve.wait_ge(flag_ps, 1)
            link(dve.tensor_reduce(flag_f[:, :], turn_ps[0:1, 0:2 * P], AX.X, ALU.max))
            link(dve.tensor_scalar(flag_f[:, :], flag_f[:, :], CMID + 0.25, None, ALU.is_gt))
            dve.tensor_copy(flag[:, :], flag_f[:, :]).then_inc(flag_ready, 1)

            def residue(c):
                tiles = slice(c * CH, (c + 1) * CH)
                dve.wait_ge(hi_ready, c + 1)
                if c >= 2:
                    dve.wait_ge(parts_ready, c - 1)
                dve.tensor_tensor(splits[c % 2], h[:, tiles, :], parts[:, 0, tiles, :], ALU.subtract).then_inc(res_ready, 1)
            dve.wait_ge(ids_t, 2)
            residue(0)
            for c in range(NCH):
                if c + 1 < NCH:
                    residue(c + 1)
                tiles = slice(c * CH, (c + 1) * CH)
                dve.wait_ge(mid_ready, c + 1)
                dve.tensor_tensor(parts[:, 2, tiles, :], splits[c % 2], parts[:, 1, tiles, :], ALU.subtract).then_inc(parts_ready, 1)

            dve.wait_ge(flag_ready, 1)
            dve.wait_ge(acc_zero, 1)
            dve.wait_ge(ids_copied, 6)
            general = dve.value_load(flag[0:1, 0:1], min_val=0, max_val=1)
            with dve.If(general):
                dve.wait_ge(g_iota, 2)
                dve.tensor_copy(g_iota_f, g_iota_i).then_inc(g_dve, 1)
                dve.wait_ge(g_dve, 1)

                for k, (v0, v1) in enumerate(GPARTS):
                    with dve.Fori(v0, v1) as v:
                        with dve.Fori(0, GSTEPS) as step:
                            n = v * GSTEPS + step
                            dve.wait_ge(g_in[k], (n - v0 * GSTEPS + 1) * 48)
                            dve.wait_ge(g_step, n + 1)
                            dve.tensor_copy(g_dst, g_dst_i).then_inc(g_dve, 1)
                            dve.wait_ge(g_dve, n + v + 2)
                            for j in range(GJ):
                                last = dve.tensor_scalar(g_hots[:, j, :], g_iota_f[0:GP, :], g_dst[:, j:j + 1], None, ALU.is_equal)
                            last.then_inc(g_hot, 1)
                        dve.wait_ge(g_closed, v + 1)
                        dve.tensor_copy(acc[:, :, ds(v * GW, GW)], win_ps[:, :, 0:GW]).then_inc(g_saved, 1)
                        dve.tensor_scalar(g_iota_f, g_iota_f, float(GW), None, ALU.add).then_inc(g_dve, 1)
                        dve.wait_ge(g_dve, (v + 1) * (GSTEPS + 1) + 1)
                dve.wait_ge(g_saved, GWINS + 1)
                dve.sem_inc(sums_ready, 1)
            with dve.Else():
                def sub_hot(n, s):
                    dve.wait_ge(subs_done, n + (SPB - HOTS + 1))
                    rel = rel_t[:, ds(n * J, J)]
                    dve.tensor_tensor(hot[:, s % HOTS, :, :], rel.unsqueeze(2).to_broadcast([P, J, WIN]),
                                      iota_f[:, :].unsqueeze(1).to_broadcast([P, J, WIN]), ALU.is_equal).then_inc(hot_ready, 1)

                def count_hot(i, q, c):
                    t = i * (RPB * TPR) + (q * RPS * TPR + c)
                    dve.wait_ge(counted, i * CPB + (q * TPR + c + 1))
                    dve.tensor_scalar(hot_lo[:, c, :], iota_h[:, 0:P], lo_t[:, ds(t, 1)], None, ALU.is_equal)
                    dve.tensor_scalar(hot_code[:, c, :], iota_h[:, :], code_t[:, ds(t, 1)], None, ALU.is_equal
                                      ).then_inc(chot_ready, 1)

                def bases(ap):
                    return nc.values_load_multi_w_load_instructions(
                        ap, engines=[dve.engine], min_val=0, max_val=N - 1,
                        skip_runtime_bounds_check_because="each is an edge's dst, which names a node")[1]

                def add_sub(i, q, s, n, base):
                    dve.wait_ge(subs_done, i * SPB + (q * SPS + s + SPB + 1))
                    dve.wait_ge(acc_step, i * (STEPS * APS) + ((q + 1) * APS + n))
                    k = 2 if s >= 2 else 1
                    o = acc[:, 0:k, ds(base, WIN)]
                    dve.tensor_tensor(o, o, win_ps[:, s % 2, 0:k * WIN].rearrange("p (k w) -> p k w", k=k), ALU.add
                                      ).then_inc(acc_step, 1)

                def add_tile(i, q, c, n, base):
                    if c == 0:
                        dve.wait_ge(applied, i * STEPS + q + 2)
                    o = acc[:, 1, ds(base, CW)]
                    dve.wait_ge(acc_step, i * (STEPS * APS) + ((q + 1) * APS + n))
                    dve.tensor_tensor(o, o, apply_ps[:, c * CW:(c + 1) * CW], ALU.add).then_inc(acc_step, 1)

                dve.sem_inc(acc_step, APS)
                for s in range(HOTS_AHEAD):
                    sub_hot(s, s)
                for c in range(TPR):
                    count_hot(0, 0, c)
                with dve.Fori(0, BODIES) as i:
                    for q in range(STEPS):
                        s0 = q * SPS
                        first = bases(tile_base[0:1, ds((i * SPB + s0) * J, SPS * J)].rearrange("a (s j) -> a s j", j=J)[:, :, 0])
                        for s in range(HOTS_AHEAD, SPS):
                            sub_hot(i * SPB + (s0 + s), s0 + s)
                        for s in range(4):
                            add_sub(i, q, s, s, first[s])
                        for c in range(TPR):
                            count_hot(i, q + 1, c)
                        for s in range(SPS, SPS + HOTS_AHEAD):
                            sub_hot(i * SPB + (s0 + s), s0 + s)
                        tiles = bases(tile_base[0:1, ds((i * RPB + q * RPS) * TPR, TPR)])
                        half = TPR // 2
                        for k in range(2):
                            for c in range(k * half, (k + 1) * half):
                                add_tile(i, q, c, 4 + k + c, tiles[c])
                            add_sub(i, q, 4 + k, 4 + (k + 1) * half + k, first[4 + k])
                dve.tensor_tensor(tail_hot[:, :, :], tail_rel[:, :].unsqueeze(2).to_broadcast([TP, TJ, WIN]),
                                  iota_f[0:TP, :].unsqueeze(1).to_broadcast([TP, TJ, WIN]), ALU.is_equal).then_inc(tail_hot_ready, 1)
                base = dve.value_load(tail_first[0:1, 0:1], min_val=0, max_val=N - 1)
                dve.wait_ge(tail_done, 1)
                dve.wait_ge(acc_step, (BODIES * STEPS + 1) * APS)
                o = acc[:, :, ds(base, WIN)]
                dve.tensor_tensor(o, o, win_ps[:, 0, 0:2 * WIN].rearrange("p (k w) -> p k w", k=2), ALU.add).then_inc(sums_ready, 1)

            for g, (t0, t1) in enumerate(groups):
                w = (t1 - t0) * F
                rows = in_use(t1 - 1)
                if g == 0:
                    dve.wait_ge(x_back[0], 16)
                if t1 > NT // 2:
                    dve.wait_ge(x_back[1], 32)
                dve.wait_ge(last_done, g + 1)
                hg = h[0:rows, t0:t1, :]
                dve.tensor_tensor(hg, count_ps[0:rows, g % 4, 0:w].rearrange("p (t f) -> p t f", f=F),
                                  b_all[0:rows, :].unsqueeze(1).to_broadcast([rows, t1 - t0, F]), ALU.add).then_inc(last_sum, 1)
                dve.wait_ge(last_sum, g + 1)
                dve.scalar_tensor_tensor(out=hg, in0=hg, scalar=0.0, in1=x_again[0:rows, t0:t1, :],
                                         op0=ALU.max, op1=ALU.add).then_inc(out_ready, 1)

        @block.tensor
        def _(pe):
            pe.wait_ge(eye, 2)
            pe.wait_ge(w_ld, 32)
            for k in range(3):
                last = pe.transpose(win_ps[:, 0, k * F:(k + 1) * F], w_in[:, k * F:(k + 1) * F], ident[:, :])
            last.then_inc(wt_ps, 1)

            def ids_out(n, c):
                return count_ps[:, n % 4, c * ROWS:(c + 1) * ROWS]
            eye_r = ident[0:ROWS, 0:ROWS]
            pe.wait_ge(dst_rel, 1)
            for q in range(2):
                view = rel_sub[:, q * SUB:(q + 1) * SUB].rearrange("r (p j) -> r j p", j=J)
                for j in range(J):
                    last = pe.transpose(ids_out(q, j), view[:, j, :], eye_r)
                last.then_inc(ids_t, 1)
            pe.wait_ge(ids_ready, 1)
            for n, arr in ((2, src_f), (3, src_f), (4, lo_f), (5, lo_f)):
                if n >= 4:
                    pe.wait_ge(ids_copied, n - 3)
                for c in range(J):
                    at = (n % 2) * J + c
                    last = pe.transpose(ids_out(n, c), arr[:, at * P:(at + 1) * P], eye_r)
                last.then_inc(ids_t, 1)
            pe.wait_ge(ids_ready, 2)
            for k in range(2):
                last = pe.transpose(turn_ps[0:1, k * P:(k + 1) * P], outside[:, k:k + 1], ident[:, :])
            last.then_inc(flag_ps, 1)

            pe.wait_ge(wt_ready, 1)
            pe.wait_ge(ids_copied, 6)

            def turn(i):
                pe.wait_ge(staged_ready, i + 1)
                pe.wait_ge(turn_copied, i + 1)
                for k in range(TURN):
                    last = pe.transpose(turn_ps[:, k * P:(k + 1) * P], staged[:, k, :], ident[:, :])
                last.then_inc(turned, 1)

            pe.wait_ge(flag_ready, 1)
            general = pe.value_load(flag[0:1, 0:1], min_val=0, max_val=1)
            pe.sem_inc(turn_copied, 1)
            pe.sem_inc(turned, 1)
            with pe.If(general):
                pe.wait_ge(parts_ready, NCH)
                with pe.Fori(0, BODIES) as i:
                    turn(i)
                pe.wait_ge(g_iota, 2)
                pe.sem_inc(g_step, 1)

                def products(m, n, g_in, g_rows):
                    pe.wait_ge(g_in, 48 * (m + 1))
                    pe.wait_ge(g_rows, 16 * GJ * (m + 1))
                    pe.wait_ge(g_hot, n + 1)
                    for j in range(GJ):
                        pe.matmul(win_ps[:, 0, 0:GW], g_edges[:, j * F:(j + 1) * F], g_hots[:, j, :], start=False, stop=False)
                        last = pe.matmul(win_ps[:, 1, 0:GW], g_gathered[:, j, :], g_hots[:, j, :], start=False, stop=False)
                    last.then_inc(g_step, 1)
                pe.sem_inc(g_saved, 1)
                for part, (v0, v1) in enumerate(GPARTS):
                    with pe.Fori(v0, v1) as v:
                        pe.wait_ge(g_saved, v + 1)
                        for k in range(2):
                            pe.matmul(win_ps[:, k, 0:GW], g_zero[:, 0:P], g_zero[:, :], start=True, stop=False)
                        with pe.Fori(0, GSTEPS) as step:
                            n = v * GSTEPS + step
                            products(n - v0 * GSTEPS, n, g_in[part], g_rows[part])
                        for k in range(2):
                            last = pe.matmul(win_ps[:, k, 0:GW], g_zero[:, 0:P], g_zero[:, :], start=False, stop=True)
                        last.then_inc(g_closed, 1)
            with pe.Else():
                pe.sem_inc(subs_done, SPB)
                pe.sem_inc(counted, CHOTS)
                pe.sem_inc(applied, 1)
                pe.sem_inc(counts_ready, 2)

                def sub_block(i, q, s):
                    r, n = q * RPS + s // 2, q * SPS + s
                    if s % 2 == 0:
                        pe.wait_ge(edges_in[r % SLOTS], i * (RPB // SLOTS * 16) + (r // SLOTS + 1) * 16)
                    pe.wait_ge(hot_ready, i * SPB + (n + 1))
                    pe.wait_ge(acc_step, i * (STEPS * APS) + (adds_through(n - 2) + APS))
                    for j in range(J):
                        last = pe.matmul(win_ps[:, n % 2, 0:WIN], edge_rows[:, r % SLOTS, s % 2, j * F:(j + 1) * F],
                                         hot[:, n % HOTS, j, :], start=j == 0, stop=j == J - 1)
                    if s >= 2:
                        k = 2 * gathered_rows(r)[1] + s % 2
                        pe.wait_ge(rows_in[k], i * (16 * J) + 16 * J)
                        for j in range(J):
                            last = pe.matmul(win_ps[:, n % 2, WIN:2 * WIN], gathered[:, k, j, :], hot[:, n % HOTS, j, :],
                                             start=j == 0, stop=j == J - 1)
                    last.then_inc(subs_done, 1)

                def count(i, q, c):
                    pe.wait_ge(chot_ready, i * CPB + (q * TPR + c + 1))
                    pe.wait_ge(counts_ready, i * CPB + (q * TPR + c + 1))
                    for k in range(2):
                        last = pe.matmul(count_ps[:, 2 * (c % 2) + k, 0:HALF], hot_lo[:, c, :],
                                         hot_code[:, c, k * HALF:(k + 1) * HALF], start=True, stop=True)
                    last.then_inc(counted, 1)

                def apply(i, q):
                    pe.wait_ge(counts_ready, i * CPB + (q + 1) * TPR + 2)
                    pe.wait_ge(parts_ready, NCH)
                    pe.wait_ge(acc_step, i * (STEPS * APS) + (adds_through(q * SPS - 1) + APS))
                    for m in range(NT * PARTS):
                        last = pe.matmul(apply_ps[:, 0:TPR * CW], parts[:, m % PARTS, m // PARTS, :],
                                         counts[:, m // PARTS, :, :].rearrange("p t w -> p (t w)"),
                                         start=m == 0, stop=m == NT * PARTS - 1)
                    last.then_inc(applied, 1)

                for c in range(EARLY):
                    count(0, 0, c)
                with pe.Fori(0, BODIES) as i:
                    for q in range(STEPS):
                        for s, (c0, c1) in enumerate(((4, 6), (6, 8), (8, 9), (9, 10))):
                            for c in range(c0, c1):
                                count(i, q, c)
                            sub_block(i, q, s)
                        apply(i, q)
                        if q == STEPS - 1:
                            turn(i)
                        for s in (4, 5):
                            for c in (2 * s - 8, 2 * s - 7):
                                count(i, q + 1, c)
                            sub_block(i, q, s)

                pe.wait_ge(tail_hot_ready, 1)
                pe.wait_ge(tail_in, 16)
                pe.wait_ge(tail_gathered, 16 * TJ)
                for j in range(TJ):
                    pe.matmul(win_ps[:, 0, 0:WIN], tail_edges[:, j * F:(j + 1) * F], tail_hot[:, j, :], start=j == 0, stop=j == TJ - 1)
                for j in range(TJ):
                    last = pe.matmul(win_ps[:, 0, WIN:2 * WIN], tail_rows[:, j, :], tail_hot[:, j, :], start=j == 0, stop=j == TJ - 1)
                last.then_inc(tail_done, 1)

            pe.wait_ge(sums_ready, 1)
            pe.wait_ge(turn_copied, BODIES + 1)
            for g, (t0, t1) in enumerate(groups):
                if g >= 4:
                    pe.wait_ge(last_sum, g - 3)
                for t in range(t0, t1):
                    rows = in_use(t)
                    o = count_ps[0:rows, g % 4, (t - t0) * F:(t - t0 + 1) * F]
                    pe.matmul(o, h[:, t, 0:rows], wt[:, 0, :], start=True, stop=False)
                    pe.matmul(o, acc[:, 0, t * P:t * P + rows], wt[:, 2, :], start=False, stop=False)
                    last = pe.matmul(o, acc[:, 1, t * P:t * P + rows], wt[:, 1, :], start=False, stop=True)
                last.then_inc(last_done, 1)


def adds_through(n):
    q, s = n // SPS, n % SPS
    return q * APS + (s + 1 if s < 4 else s + 1 + (s - 3) * (TPR // 2))


_INS = ["x", "src", "dst", "edge_attr_128", "L0_gnn_W", "L0_gnn_b"]


def kernel(**inputs):
    import numpy as np
    from concourse import bacc
    from concourse.bass_utils import run_bass_kernel_spmd

    nc = bacc.Bacc("TRN2", target_bir_lowering=False, num_devices=1)
    arrays, args = {}, []
    for name in _INS:
        a = np.ascontiguousarray(inputs[name])
        arrays[name] = a
        args.append(nc.dram_tensor(name, a.shape, mybir.dt.from_np(a.dtype), kind="ExternalInput").ap())
    out = nc.dram_tensor("out", (N, F), FP32, kind="ExternalOutput").ap()
    gnn_program(nc, *args, out)
    return run_bass_kernel_spmd(nc, [arrays], core_ids=[0]).results[0]["out"]
```

```python
from contextlib import ExitStack

import concourse.bass as bass
import concourse.mybir as mybir

FP32, BF16, FP16, I32 = mybir.dt.float32, mybir.dt.bfloat16, mybir.dt.float16, mybir.dt.int32
ALU = mybir.AluOpType
ACT = mybir.ActivationFunctionType
AX = mybir.AxisListType
ds = bass.ds

P = 128
N, E, F = 6250, 100000, 128
EPS = 1e-5

NT = -(-N // P)
NLAST = N - (NT - 1) * P
CHUNKS = [(0, 8), (8, 16), (16, 24), (24, 32), (32, 40), (40, 46), (46, NT)]
NCH = len(CHUNKS)
CH = max(t1 - t0 for t0, t1 in CHUNKS)
HI_DVE = (3, 4, 6)

J = 5
SUB = P * J
ROW = 2 * SUB
TPR = ROW // P
ROWS = E // ROW
TAIL0 = ROWS * ROW
TJ = 2
TP = (E - TAIL0) // TJ
ROWP = ROWS + 2

STEPS = 2
RPS = 3
GRPS = RPS - 1
SPS = 2 * RPS
RPB, SPB = STEPS * RPS, STEPS * SPS
GPB = STEPS * GRPS
GSLOTS = 2 * GRPS
BODIES = ROWS // RPB
assert ROWS == BODIES * RPB
CPB = STEPS * TPR
APS = SPS + TPR

WIN = 64
CW = 13
WMID, CMID = (WIN - 1) / 2, (CW - 1) / 2
HI = 50
HALF = HI // 2 * CW
PARTS = 3

SLOTS = 3
HOTS = SPS
HOTS_AHEAD = 4
SPLITS = 3
CHOTS = TPR
EARLY = 4
TURN = 4
assert TURN * BODIES >= NT and RPB % SLOTS == 0 and SPB % HOTS == 0

GW = 448
GWINS = -(-N // GW)
GP, GJ = 125, 5
GSTEPS = E // (GP * GJ)
GPARTS = [(v, min(v + 5, GWINS)) for v in range(0, GWINS, 5)]
assert 5 * GSTEPS * GJ * 16 < 2 ** 16
assert GSTEPS * GP * GJ == E
ACCW = max(GW * GWINS, N + WIN)

FB = 4


def gnn_program(nc, x, src, dst, edge, W, b, out):
    nc.disable_value_cache = True
    ctx = ExitStack()
    with ctx:
        def sb(name, shape, dt):
            return ctx.enter_context(nc.sbuf_tensor(name, shape, dt))

        def sem(name):
            return ctx.enter_context(nc.semaphore(name))

        h_dram = nc.dram_tensor("h_table", [N, PARTS * F], BF16, kind="Internal").ap()

        h = sb("h", [P, TURN * BODIES, F], FP32)
        acc = sb("acc", [P, 2, ACCW], FP32)
        parts = sb("parts", [P, NT, PARTS, F], BF16)
        staged = sb("staged", [P, TURN, F], FP32)
        counts_flat = sb("counts", [P, HI * TPR * CW], BF16)
        counts = counts_flat[:, :].rearrange("p (q t w) -> p q t w", t=TPR, w=CW)
        edge_rows = sb("edge_rows", [P, SLOTS, 2, J * F], FP32)
        gathered = sb("gathered", [P, GSLOTS, J, PARTS * F], BF16)
        gather_idx = sb("gather_idx", [P, GPB, 2, J], I32)
        hot = sb("hot", [P, HOTS, J, WIN], FP32)
        hot_bf = sb("hot_bf", [P, GSLOTS, J, WIN], BF16)
        hot_code = sb("hot_code", [P, CHOTS, 2 * HALF], BF16)
        hot_lo = sb("hot_lo", [P, CHOTS, P], BF16)
        rel_t = sb("rel_t", [P, ROWP * TPR], FP32)
        code_t = sb("code_t", [P, ROWP * TPR], FP32)
        lo_t = sb("lo_t", [P, ROWP * TPR], FP32)
        tile_base = sb("tile_base", [1, TPR * ROWS], I32)
        ident = sb("ident", [P, P], FP32)
        iota_h = sb("iota_h", [P, 2 * HALF], FP16)
        iota_f = sb("iota_f", [P, WIN], FP32)
        w_in = sb("w_in", [P, 3 * F], FP32)
        wt = sb("wt", [P, 3, F], FP32)
        b_all = sb("b_all", [P, F], FP32)
        eps = sb("eps", [P, 1], FP32)
        stats = sb("stats", [P, NT, 6], FP32)
        mv = sb("mv", [P, NT, 2], FP32)
        std = sb("std", [P, NT], FP32)
        rstd = sb("rstd", [P, NT], FP32)
        shift = sb("shift", [P, NT], FP32)
        first_sub = sb("first_sub", [ROWS, 2], FP32)
        first_tile = sb("first_tile", [ROWS, TPR], FP32)
        worst = sb("worst", [P, 2], FP32)
        outside = sb("outside", [P, 2], FP32)
        flag_f = sb("flag_f", [1, 1], FP32)
        flag = sb("flag", [1, 1], I32)
        tail_dst = sb("tail_dst", [TP, TJ], I32)
        tail_first = sb("tail_first", [TP, 1], I32)
        tail_first_f = sb("tail_first_f", [TP, 1], FP32)
        tail_rel = sb("tail_rel", [TP, TJ], FP32)
        tail_idx = sb("tail_idx", [TP, TJ], I32)
        tail_hot = sb("tail_hot", [TP, TJ, WIN], FP32)
        tail_hot_bf = sb("tail_hot_bf", [TP, TJ, WIN], BF16)
        tail_edges = stats[0:TP, :, :].rearrange("p t k -> p (t k)")[:, 0:TJ * F]
        tail_rows = w_in[0:TP, :].bitcast(BF16).rearrange("p (j f) -> p j f", j=TJ)

        lent = counts_flat[:, :].bitcast(FP32)
        rel_sub = lent[0:ROWS, 0:ROW]
        iota_i = lent[:, ROW:ROW + 2 * HALF].bitcast(I32)
        splits = gathered[:, :, :, :].rearrange("p k j f -> p (k j f)").bitcast(FP32)[:, 0:SPLITS * CH * F].rearrange(
            "p (k t f) -> p k t f", k=SPLITS, f=F)

        def split(c):
            return splits[:, c % SPLITS, 0:CHUNKS[c][1] - CHUNKS[c][0], :]
        dst_f, src_f, lo_f = (edge_rows[0:ROWS, k, :, :].rearrange("p b n -> p (b n)") for k in range(3))
        dst_i, src_i, lo_i = (v.bitcast(I32) for v in (dst_f, src_f, lo_f))

        count_ps = ctx.enter_context(nc.psum_tensor("count_ps", [P, 4, 512], FP32))
        win_ps = ctx.enter_context(nc.psum_tensor("win_ps", [P, 2, 512], FP32))
        apply_ps = ctx.enter_context(nc.psum_tensor("apply_ps", [P, 512], FP32))
        turn_ps = ctx.enter_context(nc.psum_tensor("turn_ps", [P, 512], FP32))

        x_in = [sem(f"x_in{c}") for c in range(NCH)]
        w_ld, ids_in, small_in = sem("w_ld"), sem("ids_in"), sem("small_in")
        zero_tail, consts = sem("zero_tail"), sem("consts")
        iota_done, eye = sem("iota_done"), sem("eye")
        mv_ready, std_ready, scale_ready, h_ready = (sem(n) for n in ("mv_ready", "std_ready", "scale_ready", "h_ready"))
        hi_ready, res_ready, mid_ready, parts_ready = (sem(n) for n in ("hi_ready", "res_ready", "mid_ready", "parts_ready"))
        staged_ready, turned, turn_copied = sem("staged_ready"), sem("turned"), sem("turn_copied")
        own_done, own_ready = sem("own_done"), sem("own_ready")
        h_stored = sem("h_stored")
        dve_step, pool_step, act_step = sem("dve_step"), sem("pool_step"), sem("act_step")
        dst_rel, src_ready, outside_ready = sem("dst_rel"), sem("src_ready"), sem("outside_ready")
        ids_ready, ids_t, ids_copied = sem("ids_ready"), sem("ids_t"), sem("ids_copied")
        wt_ps, wt_ready = sem("wt_ps"), sem("wt_ready")
        flag_ps, flag_ready = sem("flag_ps"), sem("flag_ready")
        acc_zero = sem("acc_zero")
        edges_in = [sem(f"edges_in{k}") for k in range(SLOTS)]
        idx_in = [sem(f"idx_in{k}") for k in range(GPB)]
        rows_in = [sem(f"rows_in{k}") for k in range(GSLOTS)]
        hot_ready, subs_done = sem("hot_ready"), sem("subs_done")
        chot_ready, counted, counts_ready = sem("chot_ready"), sem("counted"), sem("counts_ready")
        applied, acc_step = sem("applied"), sem("acc_step")
        gathers_begun = sem("gathers_begun")
        tail_in, tail_gathered, tail_hot_ready = sem("tail_in"), sem("tail_gathered"), sem("tail_hot_ready")
        tail_done, sums_ready = sem("tail_done"), sem("sums_ready")
        g_in = [sem(f"g_in{k}") for k in range(len(GPARTS))]
        g_rows = [sem(f"g_rows{k}") for k in range(len(GPARTS))]
        g_step, g_hot = sem("g_step"), sem("g_hot")
        g_iota, g_closed, g_saved = sem("g_iota"), sem("g_closed"), sem("g_saved")
        g_dve = sem("g_dve")
        x_back = [sem(f"x_back{c}") for c in range(2)]
        last_done, last_sum, out_ready, stored = (sem(n) for n in ("last_done", "last_sum", "out_ready", "stored"))

        def in_use(r):
            return P if r < NT - 1 else NLAST

        def x_tiles(v, t0, t1):
            return v[t0 * P:t1 * P, :].rearrange("(t p) f -> p t f", p=P)

        g_edges = edge_rows[0:GP, 0, 0, :]
        g_gathered = gathered[0:GP, 0, :, :]
        g_idx = gather_idx[0:GP, 2, 0, :]
        g_dst_i = gather_idx[0:GP, 2, 1, :]
        g_dst = stats[0:GP, 0, 0:GJ]
        g_iota_f = lent[:, 0:GW]
        g_hots = lent[0:GP, GW:(1 + GJ) * GW].rearrange("p (j w) -> p j w", j=GJ)
        g_hots_bf = hot_code[0:GP, :, :].rearrange("p c w -> p (c w)")[:, 0:GJ * GW].rearrange("p (j w) -> p j w", j=GJ)
        g_iota_i, g_zero = (gathered[:, k, :, :].rearrange("p j f -> p (j f)")[:, 0:2 * GW].bitcast(I32 if k == 1 else FP32)
                            for k in (1, 2))
        g_zero = g_zero[0:1, :]

        x_again = parts[:, :, :, :].rearrange("p t a f -> p (t a f)").bitcast(FP32)
        x_again = x_again[:, 0:NT * F].rearrange("p (t f) -> p t f", t=NT)
        groups = [(t, min(t + FB, NT)) for t in range(0, NT, FB)]

        def gathered_rows(r):
            return r % RPS > 0, r // RPS * GRPS + r % RPS - 1

        block = ctx.enter_context(nc.Block())

        @block.sync
        def _(sp):
            for c in range(NCH):
                t0, t1 = CHUNKS[c]
                if c < NCH - 1:
                    sp.dma_start(h[:, t0:t1, :], x_tiles(x, t0, t1)).then_inc(x_in[c], 16)
                else:
                    sp.dma_start(h[:, t0:NT - 1, :], x_tiles(x, t0, NT - 1)).then_inc(x_in[c], 16)
                    sp.wait_ge(zero_tail, 1)
                    sp.dma_start(h[0:NLAST, NT - 1, :], x[(NT - 1) * P:N, :]).then_inc(x_in[c], 16)
            sp.dma_start(tail_dst[:, :], dst[TAIL0:E].rearrange("(p j) -> p j", j=TJ)).then_inc(small_in, 16)
            sp.dma_start(tail_idx[:, :], src[TAIL0:E].rearrange("(p j) -> p j", j=TJ)).then_inc(small_in, 16)
            sp.dma_start(tail_first[:, :], dst[TAIL0:TAIL0 + 1].rearrange("(a n) -> a n", a=1).to_broadcast([TP, 1])).then_inc(small_in, 16)
            sp.dma_start(tile_base[:, :], dst[0:TAIL0].rearrange("(a s n) -> a s n", a=1, n=P)[:, :, 0],
                         allow_slow_non_contiguous=True).then_inc(small_in, 16)

            def load_indices(row, r):
                k = gathered_rows(r)[1]
                ids = src[ds(row * ROW, ROW)].rearrange("(b p j) -> p b j", b=2, j=J)
                sp.dma_start(gather_idx[:, k, :, :], ids).then_inc(idx_in[k], 16)
            ahead = [r for r in range(SLOTS) if gathered_rows(r)[0]]
            for r in ahead:
                load_indices(r, r)
            for c in range(NCH):
                sp.wait_ge(parts_ready, c + 1)
                t0, t1 = CHUNKS[c][0], min(CHUNKS[c][1], NT - 1)
                sp.dma_start(h_dram[t0 * P:t1 * P, :].rearrange("(t p) n -> p t n", p=P),
                             parts[:, t0:t1, :, :].rearrange("p t a f -> p t (a f)")).then_inc(h_stored, 16)
            sp.dma_start(h_dram[(NT - 1) * P:N, :], parts[0:NLAST, NT - 1, :, :].rearrange("p a f -> p (a f)")).then_inc(h_stored, 16)

            sp.wait_ge(flag_ready, 1)
            sp.wait_ge(ids_t, 6)
            general = sp.value_load(flag[0:1, 0:1], min_val=0, max_val=1)
            with sp.If(general):
                def load(step, n, g_in):
                    e0 = sp.snap(step * (GP * GJ))
                    sp.wait_ge(g_step, n + 1)
                    sp.dma_start(g_edges, edge[ds(e0, GP * GJ), :].rearrange("(p j) f -> p (j f)", j=GJ)).then_inc(g_in, 16)
                    sp.dma_start(g_idx, src[ds(e0, GP * GJ)].rearrange("(p j) -> p j", j=GJ)).then_inc(g_in, 16)
                    sp.dma_start(g_dst_i, dst[ds(e0, GP * GJ)].rearrange("(p j) -> p j", j=GJ)).then_inc(g_in, 16)
                for k, (v0, v1) in enumerate(GPARTS):
                    with sp.Fori(v0, v1) as v:
                        with sp.Fori(0, GSTEPS) as step:
                            load(step, v * GSTEPS + step, g_in[k])
            with sp.Else():
                sp.dma_start(tail_edges[:, :], edge[TAIL0:E, :].rearrange("(p j) f -> p (j f)", j=TJ)).then_inc(tail_in, 16)
                with sp.Fori(0, BODIES) as i:
                    for r in range(RPB):
                        row = sp.snap(i * RPB + r)
                        sp.wait_ge(subs_done, i * SPB + 2 * (r - SLOTS + 1) + SPB)
                        rows = edge[ds(row * ROW, ROW), :].rearrange("(b p j) f -> p b (j f)", b=2, j=J)
                        sp.dma_start(edge_rows[:, r % SLOTS, :, :], rows).then_inc(edges_in[r % SLOTS], 16)
                        if gathered_rows((r + SLOTS) % RPB)[0]:
                            load_indices((row + SLOTS) % ROWS, (r + SLOTS) % RPB)
                sp.wait_ge(applied, BODIES * STEPS + 1)
                sp.wait_ge(tail_gathered, 16 * TJ)
                for r in ahead:
                    sp.wait_ge(idx_in[gathered_rows(r)[1]], 16 * (BODIES + 1))

            sp.wait_ge(h_stored, 16 * (NCH + 1))
            half = NT // 2
            sp.dma_start(x_again[:, 0:half, :], x_tiles(x, 0, half)).then_inc(x_back[0], 16)
            sp.dma_start(x_again[:, half:NT - 1, :], x_tiles(x, half, NT - 1)).then_inc(x_back[1], 16)
            sp.dma_start(x_again[0:NLAST, NT - 1, :], x[(NT - 1) * P:N, :]).then_inc(x_back[1], 16)
            for g, (t0, t1) in enumerate(groups):
                sp.wait_ge(out_ready, g + 1)
                if t1 < NT:
                    sp.dma_start(x_tiles(out, t0, t1), h[:, t0:t1, :]).then_inc(stored, 16)
                else:
                    assert t1 - t0 == 1
                    sp.dma_start(out[t0 * P:N, :], h[0:NLAST, t0, :]).then_inc(stored, 16)
            sp.wait_ge(stored, 16 * len(groups))

        @block.gpsimd
        def _(pool):
            pool.memset(ident[:, :], 0.0).then_inc(eye, 1)
            pool.wait_ge(eye, 1)
            pool.affine_select(out=ident[:, :], in_=ident[:, :], compare_op=ALU.not_equal, fill=1.0, base=0,
                               pattern=[[-1, P]], channel_multiplier=1).then_inc(eye, 1)
            pool.iota(iota_i, pattern=[[1, 2 * HALF]], base=0, channel_multiplier=0).then_inc(iota_done, 1)
            pool.wait_ge(iota_done, 1)
            pool.tensor_scalar(iota_h[:, :], iota_i, -CMID, None, ALU.add).then_inc(iota_done, 1)
            pool.tensor_scalar(iota_f[:, :], iota_i[:, 0:WIN], -WMID, None, ALU.add).then_inc(iota_done, 1)
            pool.memset(acc[:, 0, :], 0.0).then_inc(acc_zero, 1)
            subs, tiles = (dst_f.rearrange("r (s n) -> r s n", n=n) for n in (SUB, P))
            pool.wait_ge(ids_in, 32)
            pool.tensor_copy(dst_f, dst_i).then_inc(pool_step, 1)
            pool.wait_ge(pool_step, 1)
            pool.tensor_scalar(first_sub[:, :], subs[:, :, 0], WMID, None, ALU.add).then_inc(pool_step, 1)
            pool.tensor_scalar(first_tile[:, :], tiles[:, :, 0], CMID, None, ALU.add).then_inc(pool_step, 1)
            pool.wait_ge(pool_step, 3)
            pool.tensor_tensor(rel_sub.rearrange("r (s n) -> r s n", n=SUB), subs,
                               first_sub[:, :].unsqueeze(2).to_broadcast([ROWS, 2, SUB]), ALU.subtract).then_inc(dst_rel, 1)
            pool.wait_ge(dst_rel, 1)
            pool.tensor_tensor(tiles, tiles, first_tile[:, :].unsqueeze(2).to_broadcast([ROWS, TPR, P]), ALU.subtract
                               ).then_inc(dst_rel, 1)
            pool.wait_ge(dst_rel, 2)
            pool.wait_ge(src_ready, 1)
            pool.tensor_tensor(src_f, src_f, dst_f, ALU.add).then_inc(ids_ready, 1)
            for c in range(NCH):
                tiles = slice(*CHUNKS[c])
                pool.wait_ge(mid_ready, c + 1)
                pool.tensor_tensor(parts[:, tiles, 2, :], split(c), parts[:, tiles, 1, :], ALU.subtract
                                   ).then_inc(parts_ready, 1)
                if c == 0:
                    pool.memset(acc[:, 1, :], 0.0).then_inc(acc_zero, 1)

            pool.wait_ge(flag_ready, 1)
            pool.wait_ge(h_stored, 16 * (NCH + 1))
            general = pool.value_load(flag[0:1, 0:1], min_val=0, max_val=1)
            with pool.If(general):
                pool.iota(g_iota_i, pattern=[[1, GW]], base=0, channel_multiplier=0).then_inc(g_iota, 1)
                pool.memset(g_zero, 0.0).then_inc(g_iota, 1)

                def gather(n, g_in, g_rows):
                    pool.wait_ge(g_in, 48 * (n + 1))
                    pool.sem_inc(gathers_begun, 1)
                    for j in range(GJ):
                        pool.indirect_dma_start(g_gathered[:, j, :], None, h_dram,
                                                bass.IndirectOffsetOnAxis(ap=g_idx[:, j:j + 1], axis=0)).then_inc(g_rows, 16)
                for k, (v0, v1) in enumerate(GPARTS):
                    with pool.Fori(0, v1 - v0) as v:
                        with pool.Fori(0, GSTEPS) as step:
                            gather(v * GSTEPS + step, g_in[k], g_rows[k])
            with pool.Else():
                with pool.Fori(0, BODIES) as i:
                    for k in range(GPB):
                        pool.wait_ge(idx_in[k], (i + 1) * 16)
                        pool.sem_inc(gathers_begun, 1)
                        for b in range(2):
                            slot = (2 * k + b) % GSLOTS
                            n = k // GRPS * SPS + 2 * (k % GRPS + 1) + b
                            pool.wait_ge(subs_done, i * SPB + (n - SPS + 1 + SPB))
                            pool.sem_inc(gathers_begun, 1)
                            for j in range(J):
                                pool.indirect_dma_start(
                                    gathered[:, slot, j, :], None, h_dram,
                                    bass.IndirectOffsetOnAxis(ap=gather_idx[:, k, b, j:j + 1], axis=0),
                                ).then_inc(rows_in[slot], 16)
                pool.wait_ge(small_in, 16 * 4)
                for j in range(TJ):
                    pool.indirect_dma_start(tail_rows[:, j, :], None, h_dram,
                                            bass.IndirectOffsetOnAxis(ap=tail_idx[:, j:j + 1], axis=0)).then_inc(tail_gathered, 16)

        @block.scalar
        def _(act):
            act.dma_start(dst_i, dst[0:TAIL0].rearrange("(r n) -> r n", n=ROW)).then_inc(ids_in, 16)
            act.dma_start(src_i, src[0:TAIL0].rearrange("(r n) -> r n", n=ROW)).then_inc(ids_in, 16)
            act.dma_start(w_in[:, :], W[:, :]).then_inc(w_ld, 16)
            act.dma_start(b_all[:, :], b.rearrange("(a n) -> a n", a=1).to_broadcast([P, F])).then_inc(w_ld, 16)
            act.wait_ge(consts, 1)
            act.activation(std[:, 0:1], eps[:, 0:1], ACT.Sqrt).then_inc(act_step, 1)
            act.wait_ge(act_step, 1)

            def root(c):
                act.wait_ge(mv_ready, c + 1)
                tiles = slice(*CHUNKS[c])
                act.activation(std[:, tiles], mv[:, tiles, 1], ACT.Sqrt, bias=eps[:, 0:1]).then_inc(std_ready, 1)

            def second_part(c):
                act.wait_ge(res_ready, c + 1)
                act.copy(parts[:, slice(*CHUNKS[c]), 1, :], split(c)).then_inc(mid_ready, 1)

            root(0)
            for c in range(NCH):
                if c + 1 < NCH:
                    root(c + 1)
                act.wait_ge(scale_ready, c + 1)
                for t in range(*CHUNKS[c]):
                    last = act.activation(h[:, t, :], h[:, t, :], ACT.Relu, bias=shift[:, t:t + 1], scale=rstd[:, t:t + 1])
                last.then_inc(h_ready, 1)
                if c not in HI_DVE:
                    act.wait_ge(h_ready, c + 1)
                    act.copy(parts[:, slice(*CHUNKS[c]), 0, :], h[:, slice(*CHUNKS[c]), :]).then_inc(hi_ready, 1)
                if c > 0:
                    second_part(c - 1)
            second_part(NCH - 1)
            act.wait_ge(wt_ps, 1)
            act.copy(wt[:, :, :], win_ps[:, 0, 0:3 * F].rearrange("p (k f) -> p k f", k=3)).then_inc(wt_ready, 1)
            for n, arr in enumerate((rel_t, rel_t, code_t, code_t, lo_t, lo_t)):
                act.wait_ge(ids_t, n + 1)
                o = arr[:, 0:ROWS * TPR].rearrange("p (r c) -> p c r", c=TPR)[:, (n % 2) * J:(n % 2) * J + J, :]
                act.copy(o, count_ps[:, n % 4, 0:J * ROWS].rearrange("p (c r) -> p c r", r=ROWS)).then_inc(ids_copied, 1)

            act.wait_ge(parts_ready, NCH)
            act.wait_ge(flag_ready, 1)
            general = act.value_load(flag[0:1, 0:1], min_val=0, max_val=1)

            def stage(i):
                act.wait_ge(own_done, i + 1)
                act.copy(staged[:, :, :], h[:, ds(i * TURN, TURN), :]).then_inc(staged_ready, 1)

            def copy_turned(i):
                act.wait_ge(turned, i + 1)
                act.copy(staged[:, :, :], turn_ps[:, :].rearrange("p (t f) -> p t f", f=F)).then_inc(turn_copied, 1)
            with act.If(general):
                with act.Fori(0, BODIES) as i:
                    stage(i)
                    copy_turned(i)
            with act.Else():
                def copy_counts(i, q, c):
                    act.wait_ge(counted, i * CPB + (q * TPR + c + 1 + CHOTS))
                    act.copy(counts[:, :, c, :].rearrange("p (a q) w -> p a q w", a=2),
                             count_ps[:, 2 * (c % 2):2 * (c % 2) + 2, 0:HALF].rearrange("p a (q w) -> p a q w", w=CW)
                             ).then_inc(counts_ready, 1)
                for c in range(EARLY):
                    copy_counts(0, 0, c)
                with act.Fori(0, BODIES) as i:
                    stage(i)
                    for q in range(STEPS):
                        for c in range(EARLY, TPR):
                            copy_counts(i, q, c)
                        act.wait_ge(applied, i * STEPS + (q + 2))
                        for c in range(EARLY):
                            copy_counts(i, q + 1, c)
                        if q == 0:
                            copy_turned(i)

        @block.vector
        def _(dve):
            steps = 0

            def link(instruction):
                nonlocal steps
                steps += 1
                instruction.then_inc(dve_step, 1)
                dve.wait_ge(dve_step, steps)

            dve.memset(h[:, NT - 1:, :], 0.0).then_inc(zero_tail, 1)
            dve.memset(eps[:, :], EPS).then_inc(consts, 1)
            dve.memset(outside[:, :], -1.0)
            dve.memset(code_t[:, ROWS * TPR:], 0.0)
            dve.memset(lo_t[:, ROWS * TPR:], 0.0)
            link(dve.memset(rel_t[:, ROWS * TPR:], 0.0))

            def moments(c):
                dve.wait_ge(x_in[c], 16 if c < NCH - 1 else 32)
                for t in range(*CHUNKS[c]):
                    last = dve.bn_stats(stats[:, t, :], h[:, t, :])
                link(last)
                for t in range(*CHUNKS[c]):
                    last = dve.bn_aggr(mv[:, t, :], stats[:, t, :])
                last.then_inc(mv_ready, 1)

            def scales(c):
                tiles = slice(*CHUNKS[c])
                dve.wait_ge(std_ready, c + 1)
                link(dve.reciprocal(rstd[:, tiles], std[:, tiles]))
                dve.scalar_tensor_tensor(out=shift[:, tiles], in0=mv[:, tiles, 0], scalar=-1.0, in1=rstd[:, tiles],
                                         op0=ALU.mult, op1=ALU.mult).then_inc(scale_ready, 1)

            def low():
                dve.wait_ge(ids_in, 32)
                link(dve.tensor_scalar(lo_i, src_i, P - 1, None, ALU.bitwise_and))

            def floats():
                dve.tensor_scalar(lo_f, lo_i, -CMID, None, ALU.add)
                link(dve.tensor_scalar(src_f, src_i, CW / P, CMID * CW / P, ALU.mult, ALU.subtract))

            def high():
                dve.scalar_tensor_tensor(out=src_f, in0=lo_f, scalar=-CW / P, in1=src_f, op0=ALU.mult, op1=ALU.add
                                         ).then_inc(src_ready, 1)

            def far_sub():
                dve.wait_ge(dst_rel, 2)
                dve.tensor_reduce(worst[0:ROWS, 0:1], rel_sub, AX.X, ALU.max, apply_absolute_value=True)

            def far_tile():
                link(dve.tensor_reduce(worst[0:ROWS, 1:2], dst_f, AX.X, ALU.max, apply_absolute_value=True))
                link(dve.scalar_tensor_tensor(out=outside[0:ROWS, 0:1], in0=worst[0:ROWS, 0:1], scalar=WMID - CMID,
                                              in1=worst[0:ROWS, 1:2], op0=ALU.subtract, op1=ALU.max))
                dve.sem_inc(outside_ready, 1)

            def far_tail():
                dve.wait_ge(small_in, 16 * 4)
                dve.tensor_copy(tail_rel[:, :], tail_dst[:, :])
                link(dve.tensor_copy(tail_first_f[:, :], tail_first[:, :]))
                link(dve.tensor_scalar(tail_rel[:, :], tail_rel[:, :], tail_first_f[:, 0:1], WMID, ALU.subtract, ALU.subtract))
                link(dve.tensor_reduce(worst[0:TP, 0:1], tail_rel[:, :], AX.X, ALU.max, apply_absolute_value=True))
                dve.tensor_scalar(outside[0:TP, 1:2], worst[0:TP, 0:1], WMID - CMID, None, ALU.subtract).then_inc(outside_ready, 1)

            def residue(c):
                tiles = slice(*CHUNKS[c])
                if c in HI_DVE:
                    dve.wait_ge(h_ready, c + 1)
                    link(dve.tensor_copy(parts[:, tiles, 0, :], h[:, tiles, :]))
                else:
                    dve.wait_ge(hi_ready, sum(k not in HI_DVE for k in range(c + 1)))
                if c >= SPLITS:
                    dve.wait_ge(parts_ready, c - SPLITS + 1)
                dve.tensor_tensor(split(c), h[:, tiles, :], parts[:, tiles, 0, :], ALU.subtract).then_inc(res_ready, 1)

            between = {0: low, 1: floats, 2: high, 5: far_tail, 6: far_sub}
            moments(0)
            for c in range(NCH):
                if c + 1 < NCH:
                    moments(c + 1)
                scales(c)
                if c in between:
                    between[c]()
                if c > 0:
                    residue(c - 1)
            far_tile()
            residue(NCH - 1)
            dve.wait_ge(flag_ps, 1)
            link(dve.tensor_reduce(flag_f[:, :], turn_ps[0:1, 0:2 * P], AX.X, ALU.max))
            link(dve.tensor_scalar(flag_f[:, :], flag_f[:, :], CMID + 0.25, None, ALU.is_gt))
            dve.tensor_copy(flag[:, :], flag_f[:, :]).then_inc(flag_ready, 1)

            dve.wait_ge(flag_ready, 1)
            dve.wait_ge(acc_zero, 2)
            dve.wait_ge(iota_done, 3)
            dve.wait_ge(ids_copied, 6)
            general = dve.value_load(flag[0:1, 0:1], min_val=0, max_val=1)

            def own_term(i):
                dve.wait_ge(own_done, i + 2)
                dve.tensor_tensor(h[:, ds(i * TURN, TURN), :], turn_ps[:, :].rearrange("p (t f) -> p t f", f=F),
                                  b_all[:, :].unsqueeze(1).to_broadcast([P, TURN, F]), ALU.add).then_inc(own_ready, 1)
            with dve.If(general):
                with dve.Fori(0, BODIES) as i:
                    own_term(i)
                dve.wait_ge(g_iota, 2)
                dve.tensor_copy(g_iota_f, g_iota_i).then_inc(g_dve, 1)
                dve.wait_ge(g_dve, 1)

                for k, (v0, v1) in enumerate(GPARTS):
                    with dve.Fori(v0, v1) as v:
                        with dve.Fori(0, GSTEPS) as step:
                            n = v * GSTEPS + step
                            dve.wait_ge(g_in[k], (n - v0 * GSTEPS + 1) * 48)
                            dve.wait_ge(g_step, n + 1)
                            dve.tensor_copy(g_dst, g_dst_i).then_inc(g_dve, 1)
                            dve.wait_ge(g_dve, n + v + 2)
                            for j in range(GJ):
                                dve.tensor_scalar(g_hots[:, j, :], g_iota_f[0:GP, :], g_dst[:, j:j + 1], None, ALU.is_equal)
                                last = dve.tensor_scalar(g_hots_bf[:, j, :], g_iota_f[0:GP, :], g_dst[:, j:j + 1], None, ALU.is_equal)
                            last.then_inc(g_hot, 1)
                        dve.wait_ge(g_closed, v + 1)
                        dve.tensor_copy(acc[:, :, ds(v * GW, GW)], win_ps[:, :, 0:GW]).then_inc(g_saved, 1)
                        dve.tensor_scalar(g_iota_f, g_iota_f, float(GW), None, ALU.add).then_inc(g_dve, 1)
                        dve.wait_ge(g_dve, (v + 1) * (GSTEPS + 1) + 1)
                dve.wait_ge(g_saved, GWINS + 1)
                dve.sem_inc(sums_ready, 1)
            with dve.Else():
                def sub_hot(n, s):
                    dve.wait_ge(subs_done, n + (SPB - HOTS + 1))
                    rel = rel_t[:, ds(n * J, J)].unsqueeze(2).to_broadcast([P, J, WIN])
                    places = iota_f[:, :].unsqueeze(1).to_broadcast([P, J, WIN])
                    last = dve.tensor_tensor(hot[:, s % SPS, :, :], rel, places, ALU.is_equal)
                    if s % SPS >= 2:
                        last = dve.tensor_tensor(hot_bf[:, s % SPS - 2, :, :], rel, places, ALU.is_equal)
                    last.then_inc(hot_ready, 1)

                def count_hot(i, q, c):
                    t = i * (RPB * TPR) + (q * RPS * TPR + c)
                    dve.wait_ge(counted, i * CPB + (q * TPR + c + 1))
                    dve.tensor_scalar(hot_lo[:, c, :], iota_h[:, 0:P], lo_t[:, ds(t, 1)], None, ALU.is_equal)
                    dve.tensor_scalar(hot_code[:, c, :], iota_h[:, :], code_t[:, ds(t, 1)], None, ALU.is_equal
                                      ).then_inc(chot_ready, 1)

                def bases(ap):
                    return nc.values_load_multi_w_load_instructions(
                        ap, engines=[dve.engine], min_val=0, max_val=N - 1,
                        skip_runtime_bounds_check_because="each is an edge's dst, which names a node")[1]

                def add_sub(i, q, s, n, base):
                    dve.wait_ge(subs_done, i * SPB + (q * SPS + s + SPB + 1))
                    dve.wait_ge(acc_step, i * (STEPS * APS) + ((q + 1) * APS + n))
                    k = 2 if s >= 2 else 1
                    o = acc[:, 0:k, ds(base, WIN)]
                    dve.tensor_tensor(o, o, win_ps[:, s % 2, 0:k * WIN].rearrange("p (k w) -> p k w", k=k), ALU.add
                                      ).then_inc(acc_step, 1)

                def add_tile(i, q, c, n, base):
                    if c == 0:
                        dve.wait_ge(applied, i * STEPS + q + 2)
                    o = acc[:, 1, ds(base, CW)]
                    dve.wait_ge(acc_step, i * (STEPS * APS) + ((q + 1) * APS + n))
                    dve.tensor_tensor(o, o, apply_ps[:, c * CW:(c + 1) * CW], ALU.add).then_inc(acc_step, 1)

                for v in (tail_hot, tail_hot_bf):
                    dve.tensor_tensor(v[:, :, :], tail_rel[:, :].unsqueeze(2).to_broadcast([TP, TJ, WIN]),
                                      iota_f[0:TP, :].unsqueeze(1).to_broadcast([TP, TJ, WIN]), ALU.is_equal).then_inc(tail_hot_ready, 1)
                for s in range(HOTS_AHEAD):
                    sub_hot(s, s)
                for c in range(TPR):
                    count_hot(0, 0, c)
                dve.sem_inc(acc_step, APS)
                with dve.Fori(0, BODIES) as i:
                    for q in range(STEPS):
                        s0 = q * SPS
                        first = bases(tile_base[0:1, ds((i * SPB + s0) * J, SPS * J)].rearrange("a (s j) -> a s j", j=J)[:, :, 0])
                        for s in range(HOTS_AHEAD, SPS):
                            sub_hot(i * SPB + (s0 + s), s0 + s)
                        for s in range(4):
                            add_sub(i, q, s, s, first[s])
                        for c in range(TPR):
                            count_hot(i, q + 1, c)
                        for s in range(SPS, SPS + HOTS_AHEAD):
                            sub_hot(i * SPB + (s0 + s), s0 + s)
                        tiles = bases(tile_base[0:1, ds((i * RPB + q * RPS) * TPR, TPR)])
                        half = TPR // 2
                        for k in range(2):
                            for c in range(k * half, (k + 1) * half):
                                add_tile(i, q, c, 4 + k + c, tiles[c])
                            add_sub(i, q, 4 + k, 4 + (k + 1) * half + k, first[4 + k])
                    own_term(i)
                base = dve.value_load(tail_first[0:1, 0:1], min_val=0, max_val=N - 1)
                dve.wait_ge(tail_done, 1)
                dve.wait_ge(acc_step, (BODIES * STEPS + 1) * APS)
                o = acc[:, :, ds(base, WIN)]
                dve.tensor_tensor(o, o, win_ps[:, 0, 0:2 * WIN].rearrange("p (k w) -> p k w", k=2), ALU.add
                                  ).then_inc(sums_ready, 1)

            dve.wait_ge(own_ready, BODIES + 1)
            for g, (t0, t1) in enumerate(groups):
                w = (t1 - t0) * F
                rows = in_use(t1 - 1)
                if g == 0:
                    dve.wait_ge(x_back[0], 16)
                if t1 > NT // 2:
                    dve.wait_ge(x_back[1], 32)
                dve.wait_ge(last_done, g + 1)
                hg = h[0:rows, t0:t1, :]
                dve.tensor_tensor(hg, hg, count_ps[0:rows, g % 4, 0:w].rearrange("p (t f) -> p t f", f=F), ALU.add
                                  ).then_inc(last_sum, 1)
                dve.wait_ge(last_sum, g + 1)
                dve.scalar_tensor_tensor(out=hg, in0=hg, scalar=0.0, in1=x_again[0:rows, t0:t1, :],
                                         op0=ALU.max, op1=ALU.add).then_inc(out_ready, 1)

        @block.tensor
        def _(pe):
            pe.wait_ge(eye, 2)
            pe.wait_ge(w_ld, 32)
            for k in range(3):
                last = pe.transpose(win_ps[:, 0, k * F:(k + 1) * F], w_in[:, k * F:(k + 1) * F], ident[:, :])
            last.then_inc(wt_ps, 1)

            def ids_out(n, c):
                return count_ps[:, n % 4, c * ROWS:(c + 1) * ROWS]
            eye_r = ident[0:ROWS, 0:ROWS]
            pe.wait_ge(dst_rel, 1)
            for q in range(2):
                view = rel_sub[:, q * SUB:(q + 1) * SUB].rearrange("r (p j) -> r j p", j=J)
                for j in range(J):
                    last = pe.transpose(ids_out(q, j), view[:, j, :], eye_r)
                last.then_inc(ids_t, 1)
            pe.wait_ge(ids_ready, 1)
            for n, arr in ((2, src_f), (3, src_f), (4, lo_f), (5, lo_f)):
                if n == 4:
                    pe.wait_ge(outside_ready, 2)
                    for k in range(2):
                        last = pe.transpose(turn_ps[0:1, k * P:(k + 1) * P], outside[:, k:k + 1], ident[:, :])
                    last.then_inc(flag_ps, 1)
                if n >= 4:
                    pe.wait_ge(ids_copied, n - 3)
                for c in range(J):
                    at = (n % 2) * J + c
                    last = pe.transpose(ids_out(n, c), arr[:, at * P:(at + 1) * P], eye_r)
                last.then_inc(ids_t, 1)
            pe.wait_ge(wt_ready, 1)
            pe.wait_ge(ids_copied, 6)

            def turn(i):
                pe.wait_ge(staged_ready, i + 1)
                pe.wait_ge(own_ready, i + 1)
                for k in range(TURN):
                    last = pe.transpose(turn_ps[:, k * P:(k + 1) * P], staged[:, k, :], ident[:, :])
                last.then_inc(turned, 1)

            def own_product(i):
                pe.wait_ge(turn_copied, i + 1)
                for k in range(TURN):
                    last = pe.matmul(turn_ps[:, k * P:(k + 1) * P], staged[:, k, :], wt[:, 0, :], start=True, stop=True)
                last.then_inc(own_done, 1)

            pe.wait_ge(flag_ready, 1)
            general = pe.value_load(flag[0:1, 0:1], min_val=0, max_val=1)
            pe.sem_inc(own_done, 1)
            pe.sem_inc(own_ready, 1)
            with pe.If(general):
                pe.wait_ge(parts_ready, NCH)
                with pe.Fori(0, BODIES) as i:
                    turn(i)
                    own_product(i)
                pe.wait_ge(g_iota, 2)
                pe.sem_inc(g_step, 1)

                def products(m, n, g_in, g_rows):
                    pe.wait_ge(g_in, 48 * (m + 1))
                    pe.wait_ge(g_rows, 16 * GJ * (m + 1))
                    pe.wait_ge(g_hot, n + 1)
                    for j in range(GJ):
                        pe.matmul(win_ps[:, 0, 0:GW], g_edges[:, j * F:(j + 1) * F], g_hots[:, j, :], start=False, stop=False)
                        for m in range(PARTS):
                            last = pe.matmul(win_ps[:, 1, 0:GW], g_gathered[:, j, m * F:(m + 1) * F], g_hots_bf[:, j, :],
                                             start=False, stop=False)
                    last.then_inc(g_step, 1)
                pe.sem_inc(g_saved, 1)
                for part, (v0, v1) in enumerate(GPARTS):
                    with pe.Fori(v0, v1) as v:
                        pe.wait_ge(g_saved, v + 1)
                        for k in range(2):
                            pe.matmul(win_ps[:, k, 0:GW], g_zero[:, 0:P], g_zero[:, :], start=True, stop=False)
                        with pe.Fori(0, GSTEPS) as step:
                            n = v * GSTEPS + step
                            products(n - v0 * GSTEPS, n, g_in[part], g_rows[part])
                        for k in range(2):
                            last = pe.matmul(win_ps[:, k, 0:GW], g_zero[:, 0:P], g_zero[:, :], start=False, stop=True)
                        last.then_inc(g_closed, 1)
            with pe.Else():
                pe.sem_inc(subs_done, SPB)
                pe.sem_inc(counted, CHOTS)
                pe.sem_inc(applied, 1)
                pe.sem_inc(counts_ready, 2)

                def sub_block(i, q, s):
                    r, n = q * RPS + s // 2, q * SPS + s
                    if s % 2 == 0:
                        pe.wait_ge(edges_in[r % SLOTS], i * (RPB // SLOTS * 16) + (r // SLOTS + 1) * 16)
                    pe.wait_ge(hot_ready, i * SPB + (n + 1))
                    pe.wait_ge(acc_step, i * (STEPS * APS) + (adds_through(n - 2) + APS))
                    for j in range(J):
                        last = pe.matmul(win_ps[:, n % 2, 0:WIN], edge_rows[:, r % SLOTS, s % 2, j * F:(j + 1) * F],
                                         hot[:, n % HOTS, j, :], start=j == 0, stop=j == J - 1)
                    if s >= 2:
                        k = s - 2
                        pe.wait_ge(rows_in[k], i * (STEPS * 16 * J) + (q + 1) * 16 * J)
                        for m in range(J * PARTS):
                            j, part = m // PARTS, m % PARTS
                            last = pe.matmul(win_ps[:, n % 2, WIN:2 * WIN], gathered[:, k, j, part * F:(part + 1) * F],
                                             hot_bf[:, k, j, :], start=m == 0, stop=m == J * PARTS - 1)
                    last.then_inc(subs_done, 1)

                def count(i, q, c):
                    pe.wait_ge(chot_ready, i * CPB + (q * TPR + c + 1))
                    pe.wait_ge(counts_ready, i * CPB + (q * TPR + c + 1))
                    for k in range(2):
                        last = pe.matmul(count_ps[:, 2 * (c % 2) + k, 0:HALF], hot_lo[:, c, :],
                                         hot_code[:, c, k * HALF:(k + 1) * HALF], start=True, stop=True)
                    last.then_inc(counted, 1)

                def apply(i, q):
                    pe.wait_ge(counts_ready, i * CPB + (q + 1) * TPR + 2)
                    pe.wait_ge(parts_ready, NCH)
                    pe.wait_ge(acc_step, i * (STEPS * APS) + (adds_through(q * SPS - 1) + APS))
                    for m in range(NT * PARTS):
                        last = pe.matmul(apply_ps[:, 0:TPR * CW], parts[:, m // PARTS, m % PARTS, :],
                                         counts[:, m // PARTS, :, :].rearrange("p t w -> p (t w)"),
                                         start=m == 0, stop=m == NT * PARTS - 1)
                    last.then_inc(applied, 1)

                for c in range(EARLY):
                    count(0, 0, c)
                with pe.Fori(0, BODIES) as i:
                    for q in range(STEPS):
                        for s, (c0, c1) in enumerate(((4, 6), (6, 8), (8, 9), (9, 10))):
                            for c in range(c0, c1):
                                count(i, q, c)
                            sub_block(i, q, s)
                        apply(i, q)
                        if q == 0:
                            turn(i)
                        else:
                            own_product(i)
                        for s in (4, 5):
                            for c in (2 * s - 8, 2 * s - 7):
                                count(i, q + 1, c)
                            sub_block(i, q, s)

                pe.wait_ge(counts_ready, BODIES * CPB + EARLY + 2)
                pe.wait_ge(acc_step, (BODIES - 1) * STEPS * APS + adds_through(SPB - 2) + APS)
                pe.wait_ge(tail_hot_ready, 2)
                pe.wait_ge(tail_in, 16)
                pe.wait_ge(tail_gathered, 16 * TJ)
                for j in range(TJ):
                    pe.matmul(win_ps[:, 0, 0:WIN], tail_edges[:, j * F:(j + 1) * F], tail_hot[:, j, :], start=j == 0, stop=j == TJ - 1)
                for m in range(TJ * PARTS):
                    j, part = m // PARTS, m % PARTS
                    last = pe.matmul(win_ps[:, 0, WIN:2 * WIN], tail_rows[:, j, part * F:(part + 1) * F], tail_hot_bf[:, j, :],
                                     start=m == 0, stop=m == TJ * PARTS - 1)
                last.then_inc(tail_done, 1)

            pe.wait_ge(sums_ready, 1)
            for g, (t0, t1) in enumerate(groups):
                if g >= 4:
                    pe.wait_ge(last_sum, g - 3)
                for t in range(t0, t1):
                    rows = in_use(t)
                    o = count_ps[0:rows, g % 4, (t - t0) * F:(t - t0 + 1) * F]
                    pe.matmul(o, acc[:, 0, t * P:t * P + rows], wt[:, 2, :], start=True, stop=False)
                    last = pe.matmul(o, acc[:, 1, t * P:t * P + rows], wt[:, 1, :], start=False, stop=True)
                last.then_inc(last_done, 1)


def adds_through(n):
    q, s = n // SPS, n % SPS
    return q * APS + (s + 1 if s < 4 else s + 1 + (s - 3) * (TPR // 2))


_INS = ["x", "src", "dst", "edge_attr_128", "L0_gnn_W", "L0_gnn_b"]


def kernel(**inputs):
    import numpy as np
    from concourse import bacc
    from concourse.bass_utils import run_bass_kernel_spmd

    nc = bacc.Bacc("TRN2", target_bir_lowering=False, num_devices=1)
    arrays, args = {}, []
    for name in _INS:
        a = np.ascontiguousarray(inputs[name])
        arrays[name] = a
        args.append(nc.dram_tensor(name, a.shape, mybir.dt.from_np(a.dtype), kind="ExternalInput").ap())
    out = nc.dram_tensor("out", (N, F), FP32, kind="ExternalOutput").ap()
    gnn_program(nc, *args, out)
    return run_bass_kernel_spmd(nc, [arrays], core_ids=[0]).results[0]["out"]
```
